# Optimizing a Trainium2 kernel written in Bass

```python
import numpy as np
import jax
import jax.numpy as jnp

def _softmax(x, axis=-1):
    return jax.nn.softmax(x, axis=axis)

def _gelu(x):
    return jax.nn.gelu(x, approximate=True)

def _silu(x):
    return jax.nn.silu(x)

def _sigmoid(x):
    return jax.nn.sigmoid(x)

def _layernorm(x, axis=-1, eps=1e-05):
    m = jnp.mean(x, axis=axis, keepdims=True)
    v = jnp.var(x, axis=axis, keepdims=True)
    return (x - m) / jnp.sqrt(v + eps)

def _scatter_add(tgt, idx, src, axis=0):
    return tgt.at[idx].add(src)

def _segment_sum(src, seg, n):
    return jax.ops.segment_sum(src, seg, n)
kernel_name = 'mk_decoder_postln_d1_seqx_r4_f95a65'

def setup_inputs(seed: int=0):
    np.random.seed(seed)
    _w = jnp.asarray

    def _rec_inputs():
        import jax
        import jax.numpy as jnp
        _rk = jax.random.key(seed)
        x = 7.22e-05 + 1 * jax.random.normal(jax.random.fold_in(_rk, 1), (4, 512, 256), jnp.float32)
        _lenS = 512 - jax.random.randint(jax.random.fold_in(_rk, 7), (4,), 0, max(1, 512 // 4) + 1, jnp.int32)
        _lenS2 = 512 - jax.random.randint(jax.random.fold_in(_rk, 8), (4,), 0, max(1, 512 // 4) + 1, jnp.int32)
        _ctx_768P = jax.random.normal(jax.random.fold_in(_rk, 11), (4, 16, 192), jnp.float32)
        _ctx_768c = jax.random.dirichlet(jax.random.fold_in(_rk, 511), 0.3 * jnp.ones((16,), jnp.float32), (4, 512))
        _ctx_768t = jnp.einsum('bsk,bkd->bsd', _ctx_768c, _ctx_768P)
        _ctx_768t = _ctx_768t * jax.lax.rsqrt(jnp.mean(jnp.square(_ctx_768t)) + 1e-12) * 0.953939
        ctx_768 = -0.000191848 + 0.999787 * (_ctx_768t + 0.3 * jax.random.normal(jax.random.fold_in(_rk, 611), (4, 512, 192), jnp.float32))
        return (x, ctx_768)
    x, ctx_768 = _rec_inputs()

    def _L0_attn_setup():
        import jax, jax.numpy as jnp
        import numpy as np
        HEADS = 16
        DIM = 256
        SPARSITY = 0.1
        key = jax.random.key(seed)
        k1, k2, k3 = jax.random.split(key, 3)
        b, n, d = (2, 512, DIM)
        inner = HEADS * 64
        x = jax.random.normal(k1, (b, n, d), dtype=jnp.float32)
        W_qkv = jax.random.normal(k2, (3 * inner, d), dtype=jnp.float32) * d ** (-0.5)
        W_out = jax.random.normal(k3, (d, inner), dtype=jnp.float32) * inner ** (-0.5)
        b_out = jnp.zeros((d,), dtype=jnp.float32)
        return {'x': x, 'W_qkv': W_qkv, 'W_out': W_out, 'b_out': b_out}
    _L0_attn_all = _L0_attn_setup()
    _L0_attn_in = {k: v for k, v in _L0_attn_all.items() if k in ('W_qkv', 'W_out', 'b_out')}
    del _L0_attn_all

    def _L0_xattn_setup():
        import jax, jax.numpy as jnp
        import numpy as np
        HEADS = 16
        DIM_HEAD = 64
        QUERY_DIM = 256
        CONTEXT_DIM = 192
        INNER = HEADS * DIM_HEAD
        SCALE = DIM_HEAD ** (-0.5)
        key = jax.random.key(seed)
        ks = jax.random.split(key, 7)
        B, Sq, Skv = (4, 512, 512)
        x = jax.random.normal(ks[0], (B, Sq, QUERY_DIM), dtype=jnp.float32)
        context = jax.random.normal(ks[1], (B, Skv, CONTEXT_DIM), dtype=jnp.float32)
        w_q = jax.random.normal(ks[2], (QUERY_DIM, INNER), dtype=jnp.float32) / np.sqrt(QUERY_DIM)
        w_k = jax.random.normal(ks[3], (CONTEXT_DIM, INNER), dtype=jnp.float32) / np.sqrt(CONTEXT_DIM)
        w_v = jax.random.normal(ks[4], (CONTEXT_DIM, INNER), dtype=jnp.float32) / np.sqrt(CONTEXT_DIM)
        w_o = jax.random.normal(ks[5], (INNER, QUERY_DIM), dtype=jnp.float32) / np.sqrt(INNER)
        b_o = jax.random.normal(ks[6], (QUERY_DIM,), dtype=jnp.float32) * 0.02
        return {'x': x, 'context': context, 'w_q': w_q, 'w_k': w_k, 'w_v': w_v, 'w_o': w_o, 'b_o': b_o}
    _L0_xattn_all = _L0_xattn_setup()
    _L0_xattn_in = {k: v for k, v in _L0_xattn_all.items() if k in ('w_q', 'w_k', 'w_v', 'w_o', 'b_o')}
    del _L0_xattn_all

    def _L0_ffn_setup():
        import jax, jax.numpy as jnp
        import numpy as np
        EPS = 1e-09
        key = jax.random.key(seed)
        k1, k2, k3, k4 = jax.random.split(key, 4)
        B, T, H, D, E = (2, 512, 256, 256, 8)
        x = jax.random.normal(k1, (B, T, H), dtype=jnp.float32)
        gate_w = jax.random.normal(k2, (E, H), dtype=jnp.float32) * 0.02
        gate_up_proj = jax.random.normal(k3, (E, H, 2 * D), dtype=jnp.float32) * 0.02
        down_proj = jax.random.normal(k4, (E, D, H), dtype=jnp.float32) * 0.02
        return {'x': x, 'gate_w': gate_w, 'gate_up_proj': gate_up_proj, 'down_proj': down_proj}
    _L0_ffn_all = _L0_ffn_setup()
    _L0_ffn_in = {k: v for k, v in _L0_ffn_all.items() if k in ('gate_w', 'gate_up_proj', 'down_proj')}
    del _L0_ffn_all
    return {'x': x, 'ctx_768': ctx_768, 'L0_attn_W_qkv': _L0_attn_in['W_qkv'], 'L0_attn_W_out': _L0_attn_in['W_out'], 'L0_attn_b_out': _L0_attn_in['b_out'], 'L0_xattn_w_q': _L0_xattn_in['w_q'], 'L0_xattn_w_k': _L0_xattn_in['w_k'], 'L0_xattn_w_v': _L0_xattn_in['w_v'], 'L0_xattn_w_o': _L0_xattn_in['w_o'], 'L0_xattn_b_o': _L0_xattn_in['b_o'], 'L0_ffn_gate_w': _L0_ffn_in['gate_w'], 'L0_ffn_gate_up_proj': _L0_ffn_in['gate_up_proj'], 'L0_ffn_down_proj': _L0_ffn_in['down_proj']}

def reference(x, ctx_768, L0_attn_W_qkv, L0_attn_W_out, L0_attn_b_out, L0_xattn_w_q, L0_xattn_w_k, L0_xattn_w_v, L0_xattn_w_o, L0_xattn_b_o, L0_ffn_gate_w, L0_ffn_gate_up_proj, L0_ffn_down_proj):
    import jax
    import jax.numpy as jnp

    def _L0_attn_ref(x, W_qkv, W_out, b_out):
        import jax, jax.numpy as jnp
        import numpy as np
        HEADS = 16
        DIM = 256
        SPARSITY = 0.1
        b, n, d = x.shape
        h = HEADS
        scale = d ** (-0.5)
        qkv = jnp.einsum('bnd,ed->bne', x, W_qkv)
        q, k, v = jnp.split(qkv, 3, axis=-1)

        def to_heads(t):
            return t.reshape(b, n, h, -1).transpose(0, 2, 1, 3)
        q, k, v = (to_heads(q), to_heads(k), to_heads(v))
        dots = jnp.einsum('bhid,bhjd->bhij', q, k) * scale
        mask_value = -jnp.finfo(dots.dtype).max
        k_top = max(1, int(SPARSITY * n))
        topk_vals, _ = jax.lax.top_k(dots, k_top)
        thresh = topk_vals[..., -1:]
        dots = jnp.where(dots >= thresh, dots, mask_value)
        v = jax.nn.relu(v)
        attn = jax.nn.softmax(dots, axis=-1)
        out = jnp.einsum('bhij,bhjd->bhid', attn, v)
        out = out.transpose(0, 2, 1, 3).reshape(b, n, -1)
        out = jnp.einsum('bne,de->bnd', out, W_out) + b_out
        return out

    def _L0_xattn_ref(x, context, w_q, w_k, w_v, w_o, b_o):
        import jax, jax.numpy as jnp
        import numpy as np
        HEADS = 16
        DIM_HEAD = 64
        QUERY_DIM = 256
        CONTEXT_DIM = 192
        INNER = HEADS * DIM_HEAD
        SCALE = DIM_HEAD ** (-0.5)
        B, Sq, _ = x.shape
        Skv = context.shape[1]
        q = (x @ w_q).reshape(B, Sq, HEADS, DIM_HEAD).transpose(0, 2, 1, 3)
        k = (context @ w_k).reshape(B, Skv, HEADS, DIM_HEAD).transpose(0, 2, 1, 3)
        v = (context @ w_v).reshape(B, Skv, HEADS, DIM_HEAD).transpose(0, 2, 1, 3)
        sim = jnp.einsum('bhid,bhjd->bhij', q, k) * SCALE
        attn = jax.nn.softmax(sim, axis=-1)
        out = jnp.einsum('bhij,bhjd->bhid', attn, v)
        out = out.transpose(0, 2, 1, 3).reshape(B, Sq, INNER)
        return out @ w_o + b_o

    def _L0_ffn_ref(x, gate_w, gate_up_proj, down_proj):
        import jax, jax.numpy as jnp
        import numpy as np
        EPS = 1e-09
        B, T, H = x.shape
        E = gate_w.shape[0]
        top_k = 2
        hidden = x.reshape(-1, H)
        router_logits = hidden @ gate_w.T
        routing_weights = jax.nn.softmax(router_logits.astype(jnp.float32), axis=-1)
        topk_weights, topk_indices = jax.lax.top_k(routing_weights, top_k)
        topk_weights = topk_weights / (jnp.sum(topk_weights, axis=-1, keepdims=True) + EPS)
        N = hidden.shape[0]
        routed = jnp.zeros((N, E), dtype=router_logits.dtype)
        rows = jnp.arange(N)[:, None]
        routed = routed.at[rows, topk_indices].set(topk_weights.astype(router_logits.dtype))
        routed = routed / (jnp.sum(routed, axis=-1, keepdims=True) + EPS)
        routed = routed.astype(hidden.dtype)
        gate_up = jnp.einsum('th,ehq->teq', hidden, gate_up_proj)
        gate, up = jnp.split(gate_up, 2, axis=-1)
        expert_outputs = jnp.einsum('teq,eqh->teh', jax.nn.silu(gate) * up, down_proj)
        out = jnp.sum(expert_outputs * routed[:, :, None], axis=1)
        return out.reshape(B, T, H)
    x = _layernorm(x + _L0_attn_ref(x, L0_attn_W_qkv, L0_attn_W_out, L0_attn_b_out), axis=-1)
    x = _layernorm(x + _L0_xattn_ref(x, ctx_768, L0_xattn_w_q, L0_xattn_w_k, L0_xattn_w_v, L0_xattn_w_o, L0_xattn_b_o), axis=-1)
    x = _layernorm(x + _L0_ffn_ref(x, L0_ffn_gate_w, L0_ffn_gate_up_proj, L0_ffn_down_proj), axis=-1)
    return x

_drawn_inputs = setup_inputs


def setup_inputs(seed=0):
    import zlib

    import numpy as np

    out = dict(_drawn_inputs(seed))
    spreads = {'L0_attn_b_out': (0.0, 0.1)}
    factors = {'L0_xattn_b_o': 3.04,
     'L0_ffn_gate_w': 5.58,
     'L0_ffn_gate_up_proj': 4.699,
     'L0_ffn_down_proj': 4.763}
    for name, (base, spread) in spreads.items():
        noise = np.random.default_rng([zlib.crc32(name.encode()), seed]).standard_normal(out[name].shape)
        drawn = base * np.exp(spread * noise) if base else spread * noise
        out[name] = jnp.asarray(drawn.astype(out[name].dtype))
    for name, factor in factors.items():
        out[name] = (out[name] * factor).astype(out[name].dtype)
    return out
```

```python
from contextlib import ExitStack

import concourse.bass as bass
from concourse import mybir

F32 = mybir.dt.float32
ALU = mybir.AluOpType
ACT = mybir.ActivationFunctionType
AX = mybir.AxisListType

P = 128
TAKEN = -3.0e38
LN_EPS = 1e-5
ROUTE_EPS = 1e-9
TOP_EXPERTS = 2


def decoder_kernel(nc, xT, x, ctxT, w_self, wo_self, bo_self, w_cross, wo_cross, bo_cross,
                   gate_wT, w_gate_up, w_down, out):
    B, DC, _, T = xT.shape
    D = x.shape[2]
    PAIRS = w_self.shape[0]
    DH = P // 2
    E = w_gate_up.shape[0]
    FC = w_down.shape[2]
    F = FC * P
    NT = T // P
    TP = 2 * NT
    CTX = ctxT.shape[1]
    CTX1 = CTX - P
    NU = B * NT
    K_TOP = max(1, int(0.1 * T))
    ROUNDS = (K_TOP + 7) // 8
    KTH = (K_TOP - 1) % 8
    SCALE = {"self": float(D) ** -0.5, "cross": float(DH) ** -0.5}

    with ExitStack() as ctx:
        def sb(name, shape):
            return ctx.enter_context(nc.sbuf_tensor(name, shape, F32))

        def psum(name, shape):
            return ctx.enter_context(nc.psum_tensor(name, shape, F32))

        def sem(name):
            return ctx.enter_context(nc.semaphore(name))

        ident = sb("ident", [P, P])
        ones_row = sb("ones_row", [1, P])
        neg_half = sb("neg_half", [P, NT])
        bo = {"self": sb("bo_s", [1, D]), "cross": sb("bo_c", [1, D])}
        wo = {"self": sb("wo_s", [P, PAIRS, D]), "cross": sb("wo_c", [P, PAIRS, D])}
        gw = sb("gw", [P, DC, E])
        x_res = sb("x_res", [P, NT, D])
        x_T = sb("x_T", [P, DC, T])
        ctx_T0 = sb("ctx_T0", [P, T])
        ctx_T1 = sb("ctx_T1", [CTX1, T])
        x1 = sb("x1", [P, NT, D])
        x1_T = sb("x1_T", [P, DC, T])
        x2_now = sb("x2_now", [P, NT, D])
        w_pair = sb("w_pair", [P, 3, 2, P])
        q_T = sb("q_T", [P, T])
        k_T = sb("k_T", [P, T])
        v_sb = sb("v_sb", [P, NT, P])
        s_sb = sb("s_sb", [P, 4, T])
        work = sb("work", [P, 2, T])
        best = sb("best", [P, ROUNDS, 8])
        neg_max = sb("neg_max", [P, 4])
        row_sum = sb("row_sum", [P, TP])
        row_inv = sb("row_inv", [P, TP])
        e_sb = sb("e_sb", [P, 2, T])
        p_sb = sb("p_sb", [P, 4, T])
        p_T = sb("p_T", [P, 2, T])
        o_sb = sb("o_sb", [P, TP, DH])
        o_T = sb("o_T", [P, PAIRS, T])
        y_sb = sb("y_sb", [P, NT, D])
        stats = sb("stats", [P, NT, 6])
        mean_var = sb("mean_var", [P, NT, 2])
        var_eps = sb("var_eps", [P, NT])
        rstd = sb("rstd", [P, NT])
        moe = sb("moe", [P, NU, D])
        x2_T = sb("x2_T", [P, DC, NU, P])
        w_gu = sb("w_gu", [P, 2, DC, 2 * F])
        w_dn = sb("w_dn", [P, 2, FC, D])
        probs = sb("probs", [P, NU, E])
        above = sb("above", [P, NU, E])
        equal = sb("equal", [P, NU, E])
        rank = sb("rank", [P, 3, NU, E])
        top8 = sb("top8", [P, NU, 8])
        col = sb("col", [P, 8, NU])
        route = sb("route", [P, NU, E])
        th = sb("th", [P, 2, F])
        hid = sb("hid", [P, 2, F])
        act_sb = sb("act_sb", [P, 2, F])
        act_T = sb("act_T", [P, 2, F])

        proj = [psum("proj0", [P, T]), psum("proj1", [P, T])]
        sc = [psum("sc0", [P, T]), psum("sc1", [P, T])]
        pt = [psum("pt0", [P, T]), psum("pt1", [P, T])]
        o_ps = psum("o_ps", [P, TP, DH])
        logits = psum("logits", [P, NU, E])

        const_loaded, ident_set, consts_set = sem("const_loaded"), sem("ident_set"), sem("consts_set")
        x_loaded, ctx_loaded, res_loaded, w_loaded = sem("x_loaded"), sem("ctx_loaded"), sem("res_loaded"), sem("w_loaded")
        qk_proj, q_ready, k_ready, v_proj, v_ready = sem("qk_proj"), sem("q_ready"), sem("k_ready"), sem("v_proj"), sem("v_ready")
        scores_ready, scores_copied, max_ready, exp_ready = sem("scores_ready"), sem("scores_copied"), sem("max_ready"), sem("exp_ready")
        probs_ready, pt_ready, pt_copied, pv_done = sem("probs_ready"), sem("pt_ready"), sem("pt_copied"), sem("pv_done")
        inv_ready, o_ready, ot_ready, ot_copied = sem("inv_ready"), sem("o_ready"), sem("ot_ready"), sem("ot_copied")
        acc_ready, vare_ready, rstd_ready, norm_ready = sem("acc_ready"), sem("vare_ready"), sem("rstd_ready"), sem("norm_ready")
        nt_ready, nt_copied, moe_started = sem("nt_ready"), sem("nt_copied"), sem("moe_started")
        search_step, norm_step, route_step = sem("search_step"), sem("norm_step"), sem("route_step")
        logits_ready, centred, rexp_ready = sem("logits_ready"), sem("centred"), sem("rexp_ready")
        experts_loaded = [sem("even_expert_loaded"), sem("odd_expert_loaded")]
        gu_ready, th_ready, hid_ready = sem("gu_ready"), sem("th_ready"), sem("hid_ready")
        act_ready, at_ready, at_copied, down_ready, moe_added = sem("act_ready"), sem("at_ready"), sem("at_copied"), sem("down_ready"), sem("moe_added")
        out_sent = sem("out_sent")
        block = ctx.enter_context(nc.Block())

        LAG_T, LAG_V = 2, 3

        def attention(eng, batch, kind, slot):
            phase = 2 * batch + (kind == "cross")
            for t in range(TP):
                slot(kind, True, phase * PAIRS, batch * PAIRS, 0, t)
            with eng.Fori(1, PAIRS) as p:
                for t in range(TP):
                    slot(kind, False, phase * PAIRS + p, batch * PAIRS + p, p, t)
            for t in range(TP, TP + LAG_V + 2):
                slot(kind, False, phase * PAIRS + PAIRS - 1, batch * PAIRS + PAIRS - 1, PAIRS - 1, t)

        def live(first, t, lag):
            return 0 <= t - lag < TP or (not first and t < lag)

        def turn_of_pair(first, t, slot):
            return t == TP + slot or (t == slot and not first)

        @block.sync
        def _(sp):
            for dst, src in ((wo["self"], wo_self), (wo["cross"], wo_cross), (bo["self"], bo_self),
                             (bo["cross"], bo_cross), (gw, gate_wT)):
                sp.dma_start(dst[:], src).then_inc(const_loaded, 16)
            with sp.Fori(0, B) as b:
                sp.wait_ge(v_proj, 2 * PAIRS * b)
                sp.dma_start(x_T[:], xT[b].rearrange("c p t -> p c t")).then_inc(x_loaded, 16)
                sp.dma_start(ctx_T0[:], ctxT[b, 0:P, :]).then_inc(ctx_loaded, 16)
                sp.dma_start(ctx_T1[:], ctxT[b, P:CTX, :]).then_inc(ctx_loaded, 16)
                sp.dma_start(x_res[:], x[b].rearrange("(n p) d -> p n d", p=P)).then_inc(res_loaded, 16)
                with sp.Fori(0, PAIRS) as p:
                    sp.wait_ge(v_proj, 2 * PAIRS * b + p)
                    sp.dma_start(w_pair[:], w_self[p]).then_inc(w_loaded, 16)
                with sp.Fori(0, PAIRS) as p:
                    sp.wait_ge(v_proj, 2 * PAIRS * b + PAIRS + p)
                    sp.dma_start(w_pair[:], w_cross[p]).then_inc(w_loaded, 16)
            with sp.Fori(0, E // 2) as ep:
                sp.wait_ge(down_ready, 2 * NU * ep)
                for k in range(2):
                    sp.dma_start(w_gu[:, k], w_gate_up[ep * 2 + k]).then_inc(experts_loaded[k], 16)
                    sp.dma_start(w_dn[:, k], w_down[ep * 2 + k]).then_inc(experts_loaded[k], 16)
            with sp.Fori(0, B) as b:
                sp.wait_ge(norm_ready, (2 * B + 1) * NT + b * NT)
                sp.dma_start(out[b].rearrange("(n p) d -> p n d", p=P), moe[:, bass.ds(b * NT, NT), :]).then_inc(out_sent, 16)
            sp.wait_ge(out_sent, 16 * B)

        @block.gpsimd
        def _(pool):
            nc.gpsimd.memset(ident[:], 0.0).then_inc(ident_set, 1)
            pool.wait_ge(ident_set, 1)
            nc.gpsimd.affine_select(out=ident[:], in_=ident[:], compare_op=ALU.not_equal, fill=1.0, base=0,
                                    pattern=[[-1, P]], channel_multiplier=1).then_inc(ident_set, 1)
            nc.gpsimd.memset(neg_half[:], -0.5).then_inc(consts_set, 1)
            nc.gpsimd.memset(ones_row[:], 1.0).then_inc(consts_set, 1)
            pool.wait_ge(consts_set, 2)

            def rsqrt(n):
                pool.wait_ge(vare_ready, n + 1)
                nc.gpsimd.tensor_tensor(rstd[:], var_eps[:], neg_half[:], ALU.pow).then_inc(rstd_ready, 1)

            with pool.Fori(0, B) as b:
                rsqrt(2 * b)
                rsqrt(2 * b + 1)
                pool.wait_ge(norm_ready, (2 * b + 2) * NT)
                nc.gpsimd.tensor_copy(moe[:, bass.ds(b * NT, NT), :], x2_now[:]).then_inc(moe_started, 1)
            with pool.Fori(0, B) as b:
                rsqrt(2 * B + b)

        @block.tensor
        def _(pe):
            def project_qk(kind, first, g):
                pe.wait_ge(w_loaded, 16 * g + 16)
                if not first:
                    pe.wait_ge(ot_copied, g - 1)
                q_in = x_T if kind == "self" else x1_T
                nc.tensor.matmul(proj[0][:], w_pair[:, 0, 0, :], q_in[:, 0, :], start=True, stop=False)
                nc.tensor.matmul(proj[0][:], w_pair[:, 0, 1, :], q_in[:, 1, :], start=False, stop=True).then_inc(qk_proj, 1)
                if kind == "self":
                    nc.tensor.matmul(proj[1][:], w_pair[:, 1, 0, :], x_T[:, 0, :], start=True, stop=False)
                    nc.tensor.matmul(proj[1][:], w_pair[:, 1, 1, :], x_T[:, 1, :], start=False, stop=True).then_inc(qk_proj, 1)
                else:
                    nc.tensor.matmul(proj[1][:], w_pair[:, 1, 0, :], ctx_T0[:], start=True, stop=False)
                    nc.tensor.matmul(proj[1][:], w_pair[0:CTX1, 1, 1, :], ctx_T1[:], start=False, stop=True).then_inc(qk_proj, 1)

            def project_v(kind, g):
                pe.wait_ge(q_ready, g + 1)
                for c in range(NT):
                    tok = slice(c * P, (c + 1) * P)
                    if kind == "self":
                        in0, in1, w1 = x_T[:, 0, tok], x_T[:, 1, tok], w_pair[:, 2, 1, :]
                    else:
                        in0, in1, w1 = ctx_T0[:, tok], ctx_T1[:, tok], w_pair[0:CTX1, 2, 1, :]
                    nc.tensor.matmul(proj[0][:, tok], in0, w_pair[:, 2, 0, :], start=True, stop=False)
                    last = nc.tensor.matmul(proj[0][:, tok], in1, w1, start=False, stop=True)
                last.then_inc(v_proj, 1)

            def slot(kind, first, g, gk, p, t):
                n = g * TP + t
                if t == 0:
                    project_qk(kind, first, g)
                if live(first, t, LAG_T):
                    pe.wait_ge(probs_ready, n - LAG_T + 1)
                    if not (first and t - LAG_T < 2):
                        pe.wait_ge(pt_copied, n - LAG_T - 1)
                    for c in range(NT):
                        last = nc.tensor.transpose(pt[t % 2][:, c * P:(c + 1) * P],
                                                   p_sb[:, (t - LAG_T) % 4, c * P:(c + 1) * P], ident[:])
                    last.then_inc(pt_ready, 1)
                if live(first, t, LAG_V):
                    h, i = (t - LAG_V) % TP // NT, (t - LAG_V) % NT
                    pe.wait_ge(pt_copied, n - LAG_V + 1)
                    if t == LAG_V:
                        pe.wait_ge(v_ready, g + 1)
                        if not first:
                            pe.wait_ge(o_ready, g)
                    for c in range(NT):
                        last = nc.tensor.matmul(o_ps[:, 2 * i + h, :], p_T[:, (t - LAG_V) % 2, c * P:(c + 1) * P],
                                                v_sb[:, c, h * DH:(h + 1) * DH], start=(c == 0), stop=(c == NT - 1))
                    last.then_inc(pv_done, 1)
                if t < TP:
                    if t == 0:
                        pe.wait_ge(q_ready, g + 1)
                        pe.wait_ge(k_ready, g + 1)
                    if not (first and t < 2):
                        if kind == "self":
                            pe.wait_ge(scores_copied, gk * TP + t - 1)
                        else:
                            pe.wait_ge(probs_ready, n - 1)
                    h, i = t // NT, t % NT
                    nc.tensor.matmul(sc[t % 2][:], q_T[h * DH:(h + 1) * DH, i * P:(i + 1) * P],
                                     k_T[h * DH:(h + 1) * DH, :], start=True, stop=True).then_inc(scores_ready, 1)
                if t == 1:
                    project_v(kind, g)
                if turn_of_pair(first, t, 3):
                    pe.wait_ge(o_ready, g if t < TP else g + 1)
                    for c in range(NT):
                        last = nc.tensor.transpose(proj[1][:, c * P:(c + 1) * P],
                                                   o_sb[:, 2 * c:2 * c + 2, :], ident[:])
                    last.then_inc(ot_ready, 1)

            def project_out(kind, phase):
                pe.wait_ge(ot_copied, (phase + 1) * PAIRS)
                for i in range(NT):
                    acc = sc[i // 2][:, (i % 2) * D:(i % 2 + 1) * D]
                    nc.tensor.matmul(acc, ones_row[:], bo[kind][:], start=True, stop=False)
                    for p in range(PAIRS):
                        last = nc.tensor.matmul(acc, o_T[:, p, i * P:(i + 1) * P], wo[kind][:, p, :],
                                                start=False, stop=(p == PAIRS - 1))
                last.then_inc(acc_ready, 1)

            def turn_rows(phase, rows):
                pe.wait_ge(norm_ready, (phase + 1) * NT)
                for c in range(DC):
                    for i in range(NT):
                        last = nc.tensor.transpose(pt[c][:, i * P:(i + 1) * P], rows[:, i, c * P:(c + 1) * P], ident[:])
                last.then_inc(nt_ready, 1)

            pe.wait_ge(ident_set, 2)
            pe.wait_ge(consts_set, 2)
            pe.wait_ge(const_loaded, 5 * 16)
            with pe.Fori(0, B) as b:
                pe.wait_ge(x_loaded, 16 * b + 16)
                attention(pe, b, "self", slot)
                project_out("self", 2 * b)
                turn_rows(2 * b, x1)
                pe.wait_ge(ctx_loaded, 32 * b + 32)
                pe.wait_ge(nt_copied, (2 * b + 1) * DC)
                attention(pe, b, "cross", slot)
                project_out("cross", 2 * b + 1)
                turn_rows(2 * b + 1, x2_now)
            pe.wait_ge(nt_copied, 2 * B * DC)
            for i in range(NU):
                for c in range(DC):
                    last = nc.tensor.matmul(logits[:, i, :], x2_T[:, c, i, :], gw[:, c, :], start=(c == 0), stop=(c == DC - 1))
            last.then_inc(logits_ready, 1)

            gate_up, turned, down = sc, pt, proj
            with pe.Fori(0, E // 2) as ep:
                for j in range(2 * NU + 2):
                    n = ep * (2 * NU) + j
                    if j < 2 * NU:
                        k, i = j // NU, j % NU
                        if i == 0:
                            pe.wait_ge(experts_loaded[k], ep * 32 + 32)
                        if j >= 2:
                            pe.wait_ge(act_ready, n - 1)
                        for c in range(DC):
                            last = nc.tensor.matmul(gate_up[j % 2][:], x2_T[:, c, i, :], w_gu[:, k, c, :],
                                                    start=(c == 0), stop=(c == DC - 1))
                        last.then_inc(gu_ready, 1)
                    if 0 <= j - 1 < 2 * NU:
                        pe.wait_ge(act_ready, n)
                        if j - 1 >= 2:
                            pe.wait_ge(at_copied, n - 2)
                        for c in range(FC):
                            last = nc.tensor.transpose(turned[(j - 1) % 2][:, c * P:(c + 1) * P],
                                                       act_sb[:, (j - 1) % 2, c * P:(c + 1) * P], ident[:])
                        last.then_inc(at_ready, 1)
                    if 0 <= j - 2 < 2 * NU:
                        k = (j - 2) // NU
                        pe.wait_ge(at_copied, n - 1)
                        if j - 2 >= 2:
                            pe.wait_ge(moe_added, n - 3)
                        for c in range(FC):
                            last = nc.tensor.matmul(down[j % 2][:, 0:D], act_T[:, j % 2, c * P:(c + 1) * P],
                                                    w_dn[:, k, c, :], start=(c == 0), stop=(c == FC - 1))
                        last.then_inc(down_ready, 1)

        @block.scalar
        def _(act):
            def slot(kind, first, g, gk, p, t):
                n = g * TP + t
                if t == 0:
                    act.wait_ge(qk_proj, 2 * g + 1)
                    if not first:
                        act.wait_ge(scores_ready, g * TP)
                    nc.scalar.copy(q_T[:], proj[0][:]).then_inc(q_ready, 1)
                    act.wait_ge(qk_proj, 2 * g + 2)
                    nc.scalar.mul(k_T[:], proj[1][:], SCALE[kind]).then_inc(k_ready, 1)
                if t < TP and kind == "self":
                    act.wait_ge(scores_ready, n + 1)
                    if not (first and t < 4):
                        act.wait_ge(probs_ready, n - 3)
                    nc.scalar.copy(s_sb[:, t % 4, :], sc[t % 2][:]).then_inc(scores_copied, 1)
                if live(first, t, 1):
                    u = (t - 1) % TP
                    act.wait_ge(max_ready, n)
                    if kind == "self":
                        if not (first and t - 1 < 2):
                            act.wait_ge(probs_ready, n - 2)
                        nc.scalar.activation(e_sb[:, u % 2, :], s_sb[:, u % 4, :], ACT.Exp,
                                             bias=neg_max[:, u % 4:u % 4 + 1], scale=1.0).then_inc(exp_ready, 1)
                    else:
                        if not (first and t - 1 < 4):
                            act.wait_ge(pt_ready, n - 4)
                        if t == 1 and not first:
                            act.wait_ge(inv_ready, g)
                        at = 2 * (u % NT) + u // NT
                        nc.scalar.activation(p_sb[:, u % 4, :], sc[u % 2][:], ACT.Exp,
                                             bias=neg_max[:, u % 4:u % 4 + 1], scale=1.0,
                                             accum_out=row_sum[:, at:at + 1]).then_inc(probs_ready, 1)
                if kind == "self" and live(first, t, LAG_T):
                    act.wait_ge(pt_ready, n - LAG_T + 1)
                    if not (first and t - LAG_T < 2):
                        act.wait_ge(pv_done, n - LAG_T - 1)
                    nc.scalar.copy(p_T[:, t % 2, :], pt[t % 2][:]).then_inc(pt_copied, 1)
                if t == 2:
                    act.wait_ge(v_proj, g + 1)
                    if not first:
                        act.wait_ge(pv_done, g * TP)
                    nc.scalar.activation(v_sb[:].rearrange("p c d -> p (c d)"), proj[0][:], ACT.Relu if kind == "self" else ACT.Copy).then_inc(v_ready, 1)
                if turn_of_pair(first, t, 4):
                    act.wait_ge(ot_ready, g if t < TP else g + 1)
                    q = p - 1 if t < TP else p
                    nc.scalar.copy(o_T[:, q, :], proj[1][:]).then_inc(ot_copied, 1)

            with act.Fori(0, B) as b:
                attention(act, b, "self", slot)
                act.wait_ge(nt_ready, 2 * b + 1)
                for c in range(DC):
                    nc.scalar.copy(x1_T[:, c, :], pt[c][:]).then_inc(nt_copied, 1)
                attention(act, b, "cross", slot)
                act.wait_ge(nt_ready, 2 * b + 2)
                for c in range(DC):
                    nc.scalar.copy(x2_T[:, c, bass.ds(b * NT, NT), :].rearrange("p n t -> p (n t)"), pt[c][:]).then_inc(nt_copied, 1)
            act.wait_ge(centred, 1)
            nc.scalar.activation(probs[:], route[:], ACT.Exp).then_inc(rexp_ready, 1)
            with act.Fori(0, E // 2) as ep:
                for j in range(2 * NU + 1):
                    n = ep * (2 * NU) + j
                    if j < 2 * NU:
                        act.wait_ge(gu_ready, n + 1)
                        if j >= 2:
                            act.wait_ge(hid_ready, n - 1)
                        nc.scalar.activation(th[:, j % 2, :], sc[j % 2][:, 0:F], ACT.Tanh, scale=0.5).then_inc(th_ready, 1)
                    if j >= 1:
                        act.wait_ge(at_ready, n)
                        if j - 1 >= 2:
                            act.wait_ge(down_ready, n - 2)
                        nc.scalar.copy(act_T[:, (j - 1) % 2, :], pt[(j - 1) % 2][:, 0:F]).then_inc(at_copied, 1)

        @block.vector
        def _(dve):
            SEARCH = 2 * ROUNDS - 1

            def hold(semaphore, value):
                value = dve.to_reg(value)
                dve.wait_ge(ident_set, 2)
                dve.wait_ge(semaphore, value)

            def kth_score(first, n, nk, u):
                hold(scores_copied, nk + 1)
                scores = s_sb[:, u % 4, :]
                for r in range(ROUNDS):
                    nc.vector.max(best[:, r, :], scores).then_inc(search_step, 1)
                    hold(search_step, nk * SEARCH + 2 * r + 1)
                    if r == 0:
                        nc.vector.tensor_scalar(neg_max[:, u % 4:u % 4 + 1], best[:, 0, 0:1], -1.0, None, ALU.mult).then_inc(max_ready, 1)
                    if r < ROUNDS - 1:
                        nc.vector.match_replace(work[:, r % 2, :], best[:, r, :], scores, TAKEN).then_inc(search_step, 1)
                        hold(search_step, nk * SEARCH + 2 * r + 2)
                        scores = work[:, r % 2, :]

            def slot(kind, first, g, gk, p, t):
                n = g * TP + t
                if kind == "cross":
                    if t < TP:
                        dve.wait_ge(scores_ready, n + 1)
                        nc.vector.tensor_reduce(neg_max[:, t % 4:t % 4 + 1], sc[t % 2][:], AX.X, ALU.max, negate=True).then_inc(max_ready, 1)
                    if live(first, t, LAG_T):
                        dve.wait_ge(pt_ready, n - LAG_T + 1)
                        if not (first and t - LAG_T < 2):
                            dve.wait_ge(pv_done, n - LAG_T - 1)
                        nc.vector.tensor_copy(p_T[:, t % 2, :], pt[t % 2][:]).then_inc(pt_copied, 1)
                elif live(first, t, 1):
                    u = (t - 1) % TP
                    at = 2 * (u % NT) + u // NT
                    kth_score(first, n - 1, gk * TP + t - 1, u)
                    dve.wait_ge(exp_ready, gk * TP + t)
                    if not (first and t - 1 < 4):
                        dve.wait_ge(pt_ready, n - 4)
                    nc.vector.scalar_tensor_tensor(out=p_sb[:, u % 4, :], in0=s_sb[:, u % 4, :],
                                                   scalar=best[:, ROUNDS - 1, KTH:KTH + 1], in1=e_sb[:, u % 2, :],
                                                   op0=ALU.is_ge, op1=ALU.mult,
                                                   accum_out=row_sum[:, at:at + 1]).then_inc(probs_ready, 1)
                if turn_of_pair(first, t, 0):
                    dve.wait_ge(probs_ready, g * TP if t < TP else (g + 1) * TP)
                    nc.vector.reciprocal(row_inv[:], row_sum[:]).then_inc(inv_ready, 1)
                if turn_of_pair(first, t, 2):
                    gn = g if t < TP else g + 1
                    dve.wait_ge(pv_done, gn * TP)
                    dve.wait_ge(inv_ready, gn)
                    dve.wait_ge(ot_ready, gn - 1)
                    nc.vector.tensor_tensor(o_sb[:], o_ps[:], row_inv[:].rearrange("p (n o) -> p n o", o=1).to_broadcast([P, TP, DH]),
                                            ALU.mult).then_inc(o_ready, 1)

            NSTEP = 2 + NT + NT

            def norm(m, add, dst):
                rows = add()
                dve.wait_ge(norm_step, m * NSTEP + 2)
                for i in range(NT):
                    nc.vector.bn_stats(stats[:, i, :], rows(i)).then_inc(norm_step, 1)
                for i in range(NT):
                    hold(norm_step, m * NSTEP + 2 + i + 1)
                    nc.vector.bn_aggr(mean_var[:, i, :], stats[:, i, :]).then_inc(norm_step, 1)
                dve.wait_ge(norm_step, m * NSTEP + NSTEP)
                nc.vector.tensor_scalar(var_eps[:], mean_var[:, :, 1], LN_EPS, None, ALU.add).then_inc(vare_ready, 1)
                dve.wait_ge(rstd_ready, m + 1)
                for i in range(NT):
                    nc.vector.tensor_scalar(dst(i), rows(i), mean_var[:, i, 0:1], rstd[:, i:i + 1],
                                            ALU.subtract, ALU.mult).then_inc(norm_ready, 1)

            def norm_attention(phase, res, dst):
                def add():
                    dve.wait_ge(acc_ready, phase + 1)
                    for j in range(2):
                        nc.vector.tensor_tensor(y_sb[:, 2 * j:2 * j + 2, :].rearrange("p n d -> p (n d)"), sc[j][:],
                                                res[:, 2 * j:2 * j + 2, :].rearrange("p n d -> p (n d)"), ALU.add).then_inc(norm_step, 1)
                    return lambda i: y_sb[:, i, :]
                norm(phase, add, lambda i: dst[:, i, :])

            with dve.Fori(0, B) as b:
                attention(dve, b, "self", slot)
                dve.wait_ge(res_loaded, 16 * b + 16)
                norm_attention(2 * b, x_res, x1)
                attention(dve, b, "cross", slot)
                dve.wait_ge(moe_started, b)
                norm_attention(2 * b + 1, x1, x2_now)

            steps = [0]

            def step(ins):
                ins.then_inc(route_step, 1)
                steps[0] += 1
                dve.wait_ge(route_step, steps[0])

            def wide(c):
                return c.rearrange("p (n o) -> p n o", o=1).to_broadcast([P, NU, E])

            dve.wait_ge(logits_ready, 1)
            step(nc.vector.tensor_reduce(col[:, 0, :], logits[:], AX.X, ALU.max))
            nc.vector.tensor_tensor(route[:], logits[:], wide(col[:, 0, :]), ALU.subtract).then_inc(centred, 1)
            dve.wait_ge(rexp_ready, 1)
            step(nc.vector.tensor_reduce(col[:, 1, :], probs[:], AX.X, ALU.add))
            step(nc.vector.reciprocal(col[:, 2, :], col[:, 1, :]))
            step(nc.vector.tensor_tensor(probs[:], probs[:], wide(col[:, 2, :]), ALU.mult))
            for i in range(NU):
                last = nc.vector.max(top8[:, i, :], probs[:, i, :])
            step(last)
            second = top8[:, :, TOP_EXPERTS - 1]
            step(nc.vector.tensor_copy(col[:, 3, :], second))
            step(nc.vector.tensor_tensor(above[:], probs[:], wide(col[:, 3, :]), ALU.is_gt))
            step(nc.vector.tensor_tensor(equal[:], probs[:], wide(col[:, 3, :]), ALU.is_equal))
            step(nc.vector.tensor_copy(rank[:, 0], equal[:]))
            shift, a = 1, 0
            while shift < E:
                step(nc.vector.tensor_copy(rank[:, (a + 1) % 3, :, 0:shift], rank[:, a, :, 0:shift]))
                step(nc.vector.tensor_tensor(rank[:, (a + 1) % 3, :, shift:E], rank[:, a, :, shift:E],
                                             rank[:, a, :, 0:E - shift], ALU.add))
                shift, a = 2 * shift, (a + 1) % 3
            step(nc.vector.tensor_reduce(col[:, 4, :], above[:], AX.X, ALU.add))
            step(nc.vector.tensor_scalar(col[:, 5, :], col[:, 4, :], -1.0, float(TOP_EXPERTS), ALU.mult, ALU.add))
            step(nc.vector.tensor_tensor(rank[:, a], rank[:, a], wide(col[:, 5, :]), ALU.is_le))
            step(nc.vector.tensor_tensor(equal[:], equal[:], rank[:, a], ALU.mult))
            step(nc.vector.tensor_tensor(above[:], above[:], equal[:], ALU.add))
            step(nc.vector.tensor_tensor(route[:], probs[:], above[:], ALU.mult))
            for again in range(2):
                step(nc.vector.tensor_reduce(col[:, 6, :], route[:], AX.X, ALU.add))
                step(nc.vector.tensor_scalar(col[:, 6, :], col[:, 6, :], ROUTE_EPS, None, ALU.add))
                step(nc.vector.reciprocal(col[:, 7, :], col[:, 6, :]))
                step(nc.vector.tensor_tensor(route[:], route[:], wide(col[:, 7, :]), ALU.mult))
            step(nc.vector.tensor_scalar(route[:], route[:], 0.5, None, ALU.mult))

            dve.wait_ge(moe_started, B)
            with dve.Fori(0, E // 2) as ep:
                for j in range(2 * NU + 2):
                    n = ep * (2 * NU) + j
                    if j < 2 * NU:
                        dve.wait_ge(th_ready, n + 1)
                        nc.vector.scalar_tensor_tensor(out=hid[:, j % 2, :], in0=th[:, j % 2, :], scalar=1.0,
                                                       in1=sc[j % 2][:, 0:F], op0=ALU.add, op1=ALU.mult).then_inc(hid_ready, 1)
                        dve.wait_ge(hid_ready, n + 1)
                        if j >= 2:
                            dve.wait_ge(at_ready, n - 1)
                        nc.vector.tensor_tensor(act_sb[:, j % 2, :], hid[:, j % 2, :], sc[j % 2][:, F:2 * F], ALU.mult).then_inc(act_ready, 1)
                    if j >= 2:
                        k, i = (j - 2) // NU, (j - 2) % NU
                        dve.wait_ge(down_ready, n - 1)
                        nc.vector.scalar_tensor_tensor(out=moe[:, i, :], in0=proj[j % 2][:, 0:D],
                                                       scalar=route[:, i, bass.ds(ep * 2 + k, 1)], in1=moe[:, i, :],
                                                       op0=ALU.mult, op1=ALU.add).then_inc(moe_added, 1)
            dve.wait_ge(moe_added, E * NU)
            with dve.Fori(0, B) as b:
                def whole():
                    dve.wait_ge(norm_ready, (2 * B + b) * NT)
                    nc.vector.tensor_copy(y_sb[:, 0:2, :], moe[:, bass.ds(b * NT, 2), :]).then_inc(norm_step, 1)
                    nc.vector.tensor_copy(y_sb[:, 2:4, :], moe[:, bass.ds(b * NT + 2, 2), :]).then_inc(norm_step, 1)
                    return lambda i: y_sb[:, i, :]
                norm(2 * B + b, whole, lambda i: moe[:, bass.ds(b * NT + i, 1), :].rearrange("p n d -> p (n d)"))


def kernel(x, ctx_768, L0_attn_W_qkv, L0_attn_W_out, L0_attn_b_out, L0_xattn_w_q, L0_xattn_w_k, L0_xattn_w_v,
           L0_xattn_w_o, L0_xattn_b_o, L0_ffn_gate_w, L0_ffn_gate_up_proj, L0_ffn_down_proj):
    import numpy as np
    import concourse.bacc as bacc
    from concourse.bass_utils import run_bass_kernel_spmd

    x, ctx_768 = np.asarray(x), np.asarray(ctx_768)
    B, T, D = x.shape
    CTX = ctx_768.shape[2]
    INNER = L0_xattn_w_q.shape[1]
    PAIRS = INNER // P

    def pair_weights(q, k, v):
        w = np.zeros((PAIRS, P, 3, 2, P), np.float32)
        for n, m in enumerate((q, k, v)):
            for c in range(2):
                rows = np.asarray(m)[c * P:(c + 1) * P]
                w[:, :rows.shape[0], n, c, :] = rows.reshape(rows.shape[0], PAIRS, P).transpose(1, 0, 2)
        return w

    qkv = np.asarray(L0_attn_W_qkv).T
    arrays = {
        "xT": x.transpose(0, 2, 1).reshape(B, D // P, P, T),
        "x": x,
        "ctxT": ctx_768.transpose(0, 2, 1),
        "w_self": pair_weights(qkv[:, :INNER], qkv[:, INNER:2 * INNER], qkv[:, 2 * INNER:]),
        "wo_self": np.asarray(L0_attn_W_out).T.reshape(PAIRS, P, D).transpose(1, 0, 2),
        "bo_self": np.asarray(L0_attn_b_out).reshape(1, D),
        "w_cross": pair_weights(L0_xattn_w_q, L0_xattn_w_k, L0_xattn_w_v),
        "wo_cross": np.asarray(L0_xattn_w_o).reshape(PAIRS, P, D).transpose(1, 0, 2),
        "bo_cross": np.asarray(L0_xattn_b_o).reshape(1, D),
        "gate_wT": np.asarray(L0_ffn_gate_w).T.reshape(D // P, P, -1).transpose(1, 0, 2),
    }
    gu, dn = np.asarray(L0_ffn_gate_up_proj), np.asarray(L0_ffn_down_proj)
    arrays["w_gate_up"] = gu.reshape(gu.shape[0], D // P, P, -1).transpose(0, 2, 1, 3)
    arrays["w_down"] = dn.reshape(dn.shape[0], dn.shape[1] // P, P, D).transpose(0, 2, 1, 3)
    arrays = {n: np.ascontiguousarray(a) for n, a in arrays.items()}
    nc = bacc.Bacc("TRN2", target_bir_lowering=False, num_devices=1)
    args = [nc.dram_tensor(n, a.shape, mybir.dt.from_np(a.dtype), kind="ExternalInput").ap() for n, a in arrays.items()]
    args.append(nc.dram_tensor("out", x.shape, F32, kind="ExternalOutput").ap())
    decoder_kernel(nc, *args)
    r = run_bass_kernel_spmd(nc, [arrays], core_ids=[0])
    return r.results[0]["out"]
```

```python
from contextlib import ExitStack

import concourse.bass as bass
from concourse import mybir

F32 = mybir.dt.float32
BF16 = mybir.dt.bfloat16
F16 = mybir.dt.float16
F32R = mybir.dt.float32r
I32 = mybir.dt.int32
ALU = mybir.AluOpType
ACT = mybir.ActivationFunctionType
AX = mybir.AxisListType

P = 128
TAKEN = -3.0e38
CUT = 2.0 ** 100
LN_EPS = 1e-5
ROUTE_EPS = 1e-9
TOP_EXPERTS = 2


def decoder_kernel(nc, xT, x, ctxT, w_self, wo_self, bo_self, w_cross, wo_cross, bo_cross,
                   gate_wT, w_gate_up, w_down, out):
    B, DC, _, T = xT.shape
    D = x.shape[2]
    PAIRS = w_self.shape[0]
    DH = P // 2
    E = w_gate_up.shape[0]
    FC = w_down.shape[2]
    F = FC * P
    NT = T // P
    TP = 2 * NT
    CTX = ctxT.shape[1]
    CTX1 = CTX - P
    NU = B * NT
    K_TOP = max(1, int(0.1 * T))
    ROUNDS = (K_TOP + 7) // 8
    KTH = (K_TOP - 1) % 8
    GT = NT
    RING = 4
    LOOPS = 2 * PAIRS // RING
    WINDOW = 16
    MIDDLE = K_TOP - WINDOW / 2 - 0.5
    FIRST_CUT = 0.6
    SLOPE = 0.9 * T / 512 / (2.2193 * 80)
    MOVES = ((1.15 * SLOPE, MIDDLE + 2.5), (0.65 * SLOPE, MIDDLE))
    P_SCALE = 2.0 ** 12
    SCALE = {"self": float(D) ** -0.5, "cross": float(DH) ** -0.5}

    with ExitStack() as ctx:
        def sb(name, shape, dt=F32):
            return ctx.enter_context(nc.sbuf_tensor(name, shape, dt))

        def psum(name, shape):
            return ctx.enter_context(nc.psum_tensor(name, shape, F32))

        def sem(name):
            return ctx.enter_context(nc.semaphore(name))

        ident = sb("ident", [P, P])
        ones_row = sb("ones_row", [1, P])
        neg_half = sb("neg_half", [P, NT])
        bo = {"self": sb("bo_s", [1, D]), "cross": sb("bo_c", [1, D])}
        wo = {"self": sb("wo_s", [P, PAIRS, D]), "cross": sb("wo_c", [P, PAIRS, D])}
        gw = sb("gw", [P, DC, E])
        x_T = sb("x_T", [P, DC, T])
        ctx_T0 = sb("ctx_T0", [P, T])
        ctx_T1 = sb("ctx_T1", [CTX1, T])
        x1 = sb("x1", [P, NT, D])
        x1_T = sb("x1_T", [P, DC, T])
        x2_now = sb("x2_now", [P, NT, D])
        w_pair = sb("w_pair", [P, 2, 3, 2, P])
        q_high, q_low = sb("q_high", [P, T], F32R), sb("q_low", [P, T], F32R)
        k_high, k_low = sb("k_high", [P, T], F32R), sb("k_low", [P, T], F32R)
        v_sb = sb("v_sb", [P, T])
        v_rest = sb("v_rest", [P, T])
        v_part = sb("v_part", [P, 2, 3, NT, P], BF16)
        neg_max = sb("neg_max", [P, 4])
        s_sb = sb("s_sb", [P, RING, GT, T])
        top8 = sb("top8", [P, RING, GT, 8])
        s_sum = sb("s_sum", [P, RING, GT])
        spread = sb("spread", [P, RING, GT])
        neg_cut = sb("neg_cut", [P, RING, 3, GT])
        sides = sb("sides", [P, RING, 3, GT])
        neg_top = sb("neg_top", [P, RING, GT])
        p_tmp = sb("p_tmp", [P, 6, GT])
        side = sb("side", [P, 2, GT, T], BF16)
        below = sb("below", [P, 2, T])
        below2 = sb("below2", [P, 2, T])
        cut_sum = sb("cut_sum", [P, RING, GT])
        next16 = sb("next16", [P, GT, WINDOW])
        place = sb("place", [P, GT])
        picked = sb("picked", [P, 2, GT, WINDOW])
        found = sb("found", [P, RING, 2, GT])
        places_i = sb("places_i", [P, GT, WINDOW], I32)
        places = sb("places", [P, GT, WINDOW])
        ones_col = sb("ones_col", [P, 1])
        row_ok = sb("row_ok", [P, GT])
        rows_ok = sb("rows_ok", [1, 8], I32)
        best = sb("best", [P, ROUNDS, 8])
        row_sum = sb("row_sum", [P, TP])
        row_inv = sb("row_inv", [P, TP])
        e_sb = sb("e_sb", [P, GT, T])
        p_sb = sb("p_sb", [P, 4, T])
        p_T = sb("p_T", [P, 2, T])
        p_high, p_low = sb("p_high", [P, 4, T], F16), sb("p_low", [P, 4, T], F16)
        o_sb = sb("o_sb", [P, TP, DH])
        o_T = sb("o_T", [P, PAIRS, T])
        y_sb = sb("y_sb", [P, NT, D])
        exact = y_sb[:].rearrange("p (a n) d -> p a (n d)", a=2)
        stats = sb("stats", [P, NT, 6])
        mean_var = sb("mean_var", [P, NT, 2])
        var_eps = sb("var_eps", [P, NT])
        rstd = sb("rstd", [P, NT])
        moe = sb("moe", [P, NU, D])
        x2_T = sb("x2_T", [P, DC, NU, P])
        s_flat = s_sb[:].rearrange("p k i t -> p (k i t)")
        w_gu = s_flat[:, 0:4 * DC * F].rearrange("p (k c f) -> p k c f", k=2, c=DC)
        w_dn = s_flat[:, 4 * DC * F:4 * DC * F + 2 * FC * D].rearrange("p (k c d) -> p k c d", k=2, c=FC)
        probs = sb("probs", [P, NU, E])
        above = sb("above", [P, NU, E])
        equal = sb("equal", [P, NU, E])
        rank = sb("rank", [P, 3, NU, E])
        r_top = sb("r_top", [P, NU, 8])
        col = sb("col", [P, 8, NU])
        route = sb("route", [P, NU, E])
        th_hid = sb("th_hid", [P, 2, 2, F])
        th, hid = th_hid[:, 0], th_hid[:, 1]
        side_unused = th_hid[:].rearrange("p a b f -> p (a b f)").bitcast(BF16).rearrange("p (i t) -> p i t", i=GT)
        act_at = 4 * DC * F + 2 * FC * D
        act_sb = s_flat[:, act_at:act_at + 2 * F].rearrange("p (k f) -> p k f", k=2)
        act_T = s_flat[:, act_at + 2 * F:act_at + 4 * F].rearrange("p (k f) -> p k f", k=2)

        proj = [psum("proj0", [P, T]), psum("proj1", [P, T])]
        sc = [psum("sc0", [P, T]), psum("sc1", [P, T])]
        pt = [psum("pt0", [P, T]), psum("pt1", [P, T])]
        o_ps = psum("o_ps", [P, TP, DH])
        logits = psum("logits", [P, NU, E])
        ok_ps = logits[0:1, 0, 0:GT]

        const_loaded, ident_set, consts_set = sem("const_loaded"), sem("ident_set"), sem("consts_set")
        x_loaded, ctx_loaded, res_loaded = sem("x_loaded"), sem("ctx_loaded"), sem("res_loaded")
        w_loaded = [sem("w_even_loaded"), sem("w_odd_loaded")]
        q_proj, k_proj, q_high_ready, k_high_ready, qk_ready = (
            sem("q_proj"), sem("k_proj"), sem("q_high_ready"), sem("k_high_ready"), sem("qk_ready"))
        v_proj, v_copied, v_first, v_rest_ready, v_second, v_ready = (
            sem("v_proj"), sem("v_copied"), sem("v_first"), sem("v_rest_ready"), sem("v_second"), sem("v_ready"))
        p_high_ready, p_ready = sem("p_high_ready"), sem("p_ready")
        scores_ready, scores_copied, max_ready, exp_ready = sem("scores_ready"), sem("scores_copied"), sem("max_ready"), sem("exp_ready")
        top_ready, cut_ready = sem("top_ready"), [sem("cut0_ready"), sem("cut1_ready"), sem("cut2_ready")]
        sides_ready = [sem("sides0_ready"), sem("sides1_ready"), sem("sides2_ready")]
        cut_step, pick_step, found_ready, ok_step, ok_ready, ok_summed, ok_read = (
            sem("cut_step"), sem("pick_step"), sem("found_ready"), sem("ok_step"), sem("ok_ready"), sem("ok_summed"), sem("ok_read"))
        probs_ready, pt_ready, pt_copied, pv_done = sem("probs_ready"), sem("pt_ready"), sem("pt_copied"), sem("pv_done")
        cut_move_step = [sem("cut1_step"), sem("cut2_step")]
        inv_ready, o_ready, ot_ready, ot_copied = sem("inv_ready"), sem("o_ready"), sem("ot_ready"), sem("ot_copied")
        acc_ready, vare_ready, rstd_ready, norm_ready = sem("acc_ready"), sem("vare_ready"), sem("rstd_ready"), sem("norm_ready")
        nt_ready, nt_copied, moe_started = sem("nt_ready"), sem("nt_copied"), sem("moe_started")
        below_step, norm_step, route_step = sem("below_step"), sem("norm_step"), sem("route_step")
        logits_ready, centred, rexp_ready = sem("logits_ready"), sem("centred"), sem("rexp_ready")
        experts_loaded = [sem("even_expert_loaded"), sem("odd_expert_loaded")]
        gu_ready, th_ready, hid_ready = sem("gu_ready"), sem("th_ready"), sem("hid_ready")
        act_ready, at_ready, at_copied, down_ready, moe_added = sem("act_ready"), sem("at_ready"), sem("at_copied"), sem("down_ready"), sem("moe_added")
        out_sent = sem("out_sent")
        block = ctx.enter_context(nc.Block())

        def stand_alone(eng, semaphore, value):
            value = eng.to_reg(value)
            eng.wait_ge(ident_set, 2)
            eng.wait_ge(semaphore, value)

        def self_attention(eng, b, period):
            def run(first, last, r, j):
                period(first, last, (2 * b) * (PAIRS * TP) + r * (RING * GT), b * (PAIRS * TP) + r * (RING * GT),
                       b * (2 * PAIRS) + r * RING, (2 * b) * PAIRS + r * (RING // 2),
                       b * PAIRS + r * (RING // 2), r, j)
            for j in range(RING):
                run(True, False, 0, j)
            with eng.Fori(1, LOOPS - 1) as r:
                for j in range(RING):
                    run(False, False, r, j)
            for j in range(2 * RING):
                run(False, True, LOOPS - 1, j)

        def due(first, j, lag):
            return 0 <= j - lag < RING or (not first and j < lag)

        LAG_T, LAG_V = 2, 4

        def cross_attention(eng, b, slot):
            def run(first, last, r, t):
                slot(first, last, (2 * b + 1) * PAIRS + r * 2, b * (PAIRS * TP) + r * (2 * TP), r, t)
            for t in range(2 * TP):
                run(True, False, 0, t)
            with eng.Fori(1, LOOPS - 1) as r:
                for t in range(2 * TP):
                    run(False, False, r, t)
            for t in range(2 * TP + LAG_V + 2):
                run(False, True, LOOPS - 1, t)

        def live(first, t, lag):
            return 0 <= t - lag < 2 * TP or (not first and t < lag)

        def after_pair(first, t, slot):
            q = (t - slot) // TP - 1
            return q if (t - slot) % TP == 0 and (q >= 0 or not first) and -2 <= q < 2 and t >= slot else None

        @block.sync
        def _(sp):
            def load_inputs(b):
                sp.dma_start(x_T[:], xT[b].rearrange("c p t -> p c t")).then_inc(x_loaded, 16)
                sp.dma_start(ctx_T0[:], ctxT[b, 0:P, :]).then_inc(ctx_loaded, 16)
                sp.dma_start(ctx_T1[:], ctxT[b, P:CTX, :]).then_inc(ctx_loaded, 16)

            def load_rows(b):
                sp.dma_start(x1[:], x[b].rearrange("(n p) d -> p n d", p=P)).then_inc(res_loaded, 16)

            def load_pairs(w, g, r):
                for k in range(2):
                    sp.wait_ge(v_proj, g + k - 1)
                    sp.dma_start(w_pair[:, k], w[r * 2 + k]).then_inc(w_loaded[k], 16)

            def load_experts(ep):
                for k in range(2):
                    sp.dma_start(w_gu[:, k], w_gate_up[ep * 2 + k]).then_inc(experts_loaded[k], 16)
                    sp.dma_start(w_dn[:, k], w_down[ep * 2 + k]).then_inc(experts_loaded[k], 16)

            sp.dma_start(w_pair[:, 0], w_self[0]).then_inc(w_loaded[0], 16)
            load_inputs(0)
            sp.dma_start(w_pair[:, 1], w_self[1]).then_inc(w_loaded[1], 16)
            for dst, src in ((wo["self"], wo_self), (wo["cross"], wo_cross), (bo["self"], bo_self),
                             (bo["cross"], bo_cross), (gw, gate_wT)):
                sp.dma_start(dst[:], src).then_inc(const_loaded, 16)
            load_rows(0)
            with sp.Fori(1, PAIRS // 2) as r:
                load_pairs(w_self, r * 2, r)
            with sp.Fori(0, PAIRS // 2) as r:
                load_pairs(w_cross, r * 2 + PAIRS, r)
            with sp.Fori(1, B) as b:
                sp.wait_ge(v_proj, 2 * PAIRS * b)
                load_inputs(b)
                load_pairs(w_self, b * (2 * PAIRS), 0)
                sp.wait_ge(norm_ready, 2 * NT * b)
                load_rows(b)
                with sp.Fori(1, PAIRS // 2) as r:
                    load_pairs(w_self, b * (2 * PAIRS) + r * 2, r)
                with sp.Fori(0, PAIRS // 2) as r:
                    load_pairs(w_cross, b * (2 * PAIRS) + r * 2 + PAIRS, r)
            sp.wait_ge(norm_ready, (2 * B - 1) * NT)
            load_experts(0)
            with sp.Fori(1, E // 2) as ep:
                sp.wait_ge(down_ready, 2 * NU * ep)
                load_experts(ep)
            with sp.Fori(0, B) as b:
                sp.wait_ge(norm_ready, (2 * B + 1) * NT + b * NT)
                sp.dma_start(out[b].rearrange("(n p) d -> p n d", p=P), moe[:, bass.ds(b * NT, NT), :]).then_inc(out_sent, 16)
            sp.wait_ge(out_sent, 16 * B)

        @block.gpsimd
        def _(pool):
            nc.gpsimd.memset(ident[:], 0.0).then_inc(ident_set, 1)
            pool.wait_ge(ident_set, 1)
            nc.gpsimd.affine_select(out=ident[:], in_=ident[:], compare_op=ALU.not_equal, fill=1.0, base=0,
                                    pattern=[[-1, P]], channel_multiplier=1).then_inc(ident_set, 1)
            nc.gpsimd.memset(neg_half[:], -0.5).then_inc(consts_set, 1)
            nc.gpsimd.memset(ones_row[:], 1.0).then_inc(consts_set, 1)
            nc.gpsimd.memset(ones_col[:], 1.0).then_inc(consts_set, 1)
            nc.gpsimd.iota(places_i[:], [[0, GT], [1, WINDOW]], base=0, channel_multiplier=0).then_inc(consts_set, 1)
            pool.wait_ge(consts_set, 4)
            nc.gpsimd.tensor_copy(places[:], places_i[:]).then_inc(consts_set, 1)
            pool.wait_ge(consts_set, 5)

            TS, TT = nc.gpsimd.tensor_scalar, nc.gpsimd.tensor_tensor

            def move_cut(ns, gg, j, c):
                s_step = cut_move_step[c]
                stand_alone(pool, sides_ready[c], ns)
                TS(p_tmp[:, 2 * c + 2, :], sides[:, j, c, :], T - 2 * MOVES[c][1], -MOVES[c][0] / 2, ALU.add, ALU.mult).then_inc(s_step, 1)
                pool.wait_ge(s_step, 2 * gg - 1)
                TT(p_tmp[:, 2 * c + 3, :], p_tmp[:, 2 * c + 2, :], spread[:, j, :], ALU.mult).then_inc(s_step, 1)
                pool.wait_ge(s_step, 2 * gg)
                TT(neg_cut[:, j, c + 1, :], neg_cut[:, j, c, :], p_tmp[:, 2 * c + 3, :], ALU.add).then_inc(cut_ready[c + 1], 1)

            def split_probs(n, ns, i, fresh):
                stand_alone(pool, pt_copied, ns + 1)
                if not fresh:
                    stand_alone(pool, pv_done, n - 3)
                TS(p_high[:, i, :], p_T[:, i % 2, :], 1.0, 0.0, ALU.mult, ALU.add).then_inc(p_high_ready, 1)
                pool.wait_ge(p_high_ready, n + 1)
                TT(p_low[:, i, :], p_T[:, i % 2, :], p_high[:, i, :], ALU.subtract).then_inc(p_ready, 1)

            def value_part(q, k):
                return v_part[:, q, k].rearrange("p c d -> p (c d)")

            def first_value_part(g, gs, q):
                stand_alone(pool, v_copied, g + 1)
                TS(value_part(q, 0), v_sb[:], 1.0, 0.0, ALU.mult, ALU.add).then_inc(v_first, 1)
                pool.wait_ge(v_first, gs + 1)
                TT(v_rest[:], v_sb[:], value_part(q, 0), ALU.subtract).then_inc(v_rest_ready, 1)

            def last_value_parts(g, q):
                stand_alone(pool, v_rest_ready, g + 1)
                TS(value_part(q, 1), v_rest[:], 1.0, 0.0, ALU.mult, ALU.add).then_inc(v_second, 1)
                pool.wait_ge(v_second, g + 1)
                TT(value_part(q, 2), v_rest[:], value_part(q, 1), ALU.subtract).then_inc(v_ready, 1)

            def first_cut(ns, gg, j):
                stand_alone(pool, top_ready, ns)
                stand_alone(pool, scores_copied, ns)
                TS(neg_top[:, j, :], top8[:, j, :, 0], -1.0, None, ALU.mult).then_inc(cut_step, 1)
                TS(p_tmp[:, 0, :], s_sum[:, j, :], 1.0 / T, None, ALU.mult).then_inc(cut_step, 1)
                pool.wait_ge(cut_step, 4 * gg - 2)
                TT(spread[:, j, :], top8[:, j, :, 7], p_tmp[:, 0, :], ALU.subtract).then_inc(cut_step, 1)
                stand_alone(pool, cut_step, 4 * gg - 1)
                TS(p_tmp[:, 1, :], spread[:, j, :], -FIRST_CUT, None, ALU.mult).then_inc(cut_step, 1)
                pool.wait_ge(cut_step, 4 * gg)
                TT(neg_cut[:, j, 0, :], p_tmp[:, 1, :], p_tmp[:, 0, :], ALU.subtract).then_inc(cut_ready[0], 1)

            def judge(gg, j, fresh):
                stand_alone(pool, found_ready, gg)
                TS(p_tmp[:, 4, :], cut_sum[:, j, :], 2.0 / CUT, float(T), ALU.mult, ALU.add).then_inc(ok_step, 1)
                pool.wait_ge(ok_step, 3 * gg - 2)
                TT(p_tmp[:, 5, :], p_tmp[:, 4, :], sides[:, j, 2, :], ALU.add).then_inc(ok_step, 1)
                stand_alone(pool, ok_step, 3 * gg - 1)
                TS(p_tmp[:, 4, :], p_tmp[:, 5, :], 0.0, None, ALU.is_equal).then_inc(ok_step, 1)
                pool.wait_ge(ok_step, 3 * gg)
                if not fresh:
                    pool.wait_ge(ok_summed, gg - 1)
                TT(row_ok[:], p_tmp[:, 4, :], found[:, j, 0, :], ALU.mult).then_inc(ok_ready, 1)

            def period(first, last, nb, ns, gg, g, gs, r, j):
                new, cuts, low, old = (due(first, j, lag) for lag in range(4))

                def split(i):
                    split_probs(nb + (j - 3) * GT + i, ns + (j - 3) * GT + i, i, first and j == 3)

                if cuts:
                    move_cut(ns + j * GT, gg + j, (j - 1) % RING, 0)
                if old:
                    split(0)
                    split(1)
                if cuts:
                    move_cut(ns + j * GT, gg + j, (j - 1) % RING, 1)
                if old:
                    split(2)
                if low:
                    judge(gg + (j - 1), (j - 2) % RING, first and j == 2)
                if old:
                    split(3)
                if new:
                    first_cut(ns + (j + 1) * GT, gg + (j + 1), j)
                if new and j % 2 == 1:
                    first_value_part(g + j // 2, gs + j // 2, j // 2)
                    last_value_parts(g + j // 2, j // 2)

            def slot(first, last, g, nx, r, t):
                if t < 2 * TP and t % TP == 2:
                    last_value_parts(g + t // TP, t // TP)

            def rsqrt(n):
                pool.wait_ge(vare_ready, n + 1)
                nc.gpsimd.tensor_tensor(rstd[:], var_eps[:], neg_half[:], ALU.pow).then_inc(rstd_ready, 1)

            with pool.Fori(0, B) as b:
                self_attention(pool, b, period)
                rsqrt(2 * b)
                cross_attention(pool, b, slot)
                rsqrt(2 * b + 1)
                pool.wait_ge(norm_ready, (2 * b + 2) * NT)
                nc.gpsimd.tensor_copy(moe[:, bass.ds(b * NT, NT), :], x2_now[:]).then_inc(moe_started, 1)
                pool.wait_ge(moe_started, b + 1)
            with pool.Fori(0, B) as b:
                rsqrt(2 * B + b)

        @block.tensor
        def _(pe):
            def project_qk(kind, g, q, turned=None):
                pe.wait_ge(w_loaded[q], 8 * (g - q) + 16)
                w = w_pair[:, q]
                q_in = x_T if kind == "self" else x1_T
                nc.tensor.matmul(proj[0][:], w[:, 0, 0, :], q_in[:, 0, :], start=True, stop=False)
                nc.tensor.matmul(proj[0][:], w[:, 0, 1, :], q_in[:, 1, :], start=False, stop=True).then_inc(q_proj, 1)
                if turned is not None:
                    pe.wait_ge(ot_copied, turned)
                if kind == "self":
                    nc.tensor.matmul(proj[1][:], w[:, 1, 0, :], x_T[:, 0, :], start=True, stop=False)
                    nc.tensor.matmul(proj[1][:], w[:, 1, 1, :], x_T[:, 1, :], start=False, stop=True).then_inc(k_proj, 1)
                else:
                    nc.tensor.matmul(proj[1][:], w[:, 1, 0, :], ctx_T0[:], start=True, stop=False)
                    nc.tensor.matmul(proj[1][:], w[0:CTX1, 1, 1, :], ctx_T1[:], start=False, stop=True).then_inc(k_proj, 1)

            def project_v(kind, q):
                w = w_pair[:, q]
                for c in range(NT):
                    tok = slice(c * P, (c + 1) * P)
                    if kind == "self":
                        in0, in1, w1 = x_T[:, 0, tok], x_T[:, 1, tok], w[:, 2, 1, :]
                    else:
                        in0, in1, w1 = ctx_T0[:, tok], ctx_T1[:, tok], w[0:CTX1, 2, 1, :]
                    nc.tensor.matmul(proj[0][:, tok], in0, w[:, 2, 0, :], start=True, stop=False)
                    last = nc.tensor.matmul(proj[0][:, tok], in1, w1, start=False, stop=True)
                last.then_inc(v_proj, 1)

            def scores(bank, h, i):
                rows, cols = slice(h * DH, (h + 1) * DH), slice(i * P, (i + 1) * P)
                nc.tensor.matmul(bank[:], q_low[rows, cols], k_high[rows, :], start=True, stop=False)
                nc.tensor.matmul(bank[:], q_high[rows, cols], k_low[rows, :], start=False, stop=False)
                nc.tensor.matmul(bank[:], q_high[rows, cols], k_high[rows, :], start=False, stop=True).then_inc(scores_ready, 1)

            def transpose_probs(bank, probs_tile):
                for c in range(NT):
                    last = nc.tensor.transpose(bank[:, c * P:(c + 1) * P], probs_tile[:, c * P:(c + 1) * P], ident[:])
                last.then_inc(pt_ready, 1)

            def weigh_values(h, i, k, q):
                for c in range(NT):
                    at = slice(c * P, (c + 1) * P)
                    values = [v_part[:, q, m, c, h * DH:(h + 1) * DH] for m in range(3)]
                    for probs_part, value_part in ((p_low, 1), (p_low, 0), (p_high, 2), (p_high, 1), (p_high, 0)):
                        last = nc.tensor.matmul(o_ps[:, 2 * i + h, :], probs_part[:, k, at], values[value_part],
                                                start=(c == 0 and probs_part is p_low and value_part == 1),
                                                stop=(c == NT - 1 and probs_part is p_high and value_part == 0))
                last.then_inc(pv_done, 1)

            def turn_outputs():
                for c in range(NT):
                    last = nc.tensor.transpose(proj[1][:, c * P:(c + 1) * P], o_sb[:, 2 * c:2 * c + 2, :], ident[:])
                last.then_inc(ot_ready, 1)

            def period(first, last, nb, ns, gg, g, gs, r, j):
                def tile(lag, i):
                    return (j - lag) * GT + i

                def scores_of(i):
                    if not (first and j == 0 and i < 2):
                        pe.wait_ge(scores_copied, ns + tile(0, i) - 1)
                    scores(sc[i % 2], j % 2, i)

                def turn(i):
                    pe.wait_ge(probs_ready, nb + tile(3, i) + 1)
                    if not (first and j == 3 and i < 2):
                        pe.wait_ge(pt_copied, ns + tile(3, i) - 1)
                    transpose_probs(pt[i % 2], p_sb[:, i, :])

                def weigh(lag, i):
                    pe.wait_ge(p_ready, nb + tile(lag, i) + 1)
                    weigh_values((j - lag) % 2, i, i, (j - lag) % RING // 2)

                new, old = due(first, j, 0), due(first, j, 3)
                if first and j == 0:
                    project_qk("self", g, 0)
                if old:
                    pe.wait_ge(ok_ready, gg + (j - 2))
                    nc.tensor.matmul(ok_ps, ones_col[:], row_ok[:], start=True, stop=True).then_inc(ok_summed, 1)
                if new:
                    if j % 2 == 0:
                        pe.wait_ge(qk_ready, (g + j // 2) * 2 + 2)
                    scores_of(0)
                    scores_of(1)
                if due(first, j, 4):
                    weigh(4, 2)
                    weigh(4, 3)
                if old:
                    turn(0)
                    turn(1)
                if new:
                    scores_of(2)
                    scores_of(3)
                    if j % 2 == 1:
                        project_v("self", j // 2)
                if old:
                    turn(2)
                    turn(3)
                ended = j % 2 == 1 and due(first, j - 1, 4)
                if ended:
                    pe.wait_ge(o_ready, g + (j - 3) // 2)
                    turn_outputs()
                if new and j % 2 == 1:
                    pe.wait_ge(v_copied, g + j // 2 + 1)
                    if not (last and j == RING - 1):
                        project_qk("self", g + j // 2 + 1, (j // 2 + 1) % 2, g + (j - 3) // 2 if ended else None)
                if ended and not new:
                    pe.wait_ge(ot_copied, g + (j - 3) // 2)
                if old:
                    if j % 2 == 1:
                        pe.wait_ge(v_ready, g + (j - 3) // 2 + 1)
                        if ended:
                            pe.wait_ge(o_ready, g + (j - 3) // 2)
                    weigh(3, 0)
                    weigh(3, 1)

            def slot(first, last, g, nx, r, t):
                n = g * TP + t
                if first and t == 0:
                    project_qk("cross", g, 0)
                if live(first, t, LAG_T):
                    pe.wait_ge(probs_ready, n - LAG_T + 1)
                    if not (first and t - LAG_T < 2):
                        pe.wait_ge(p_ready, n - LAG_T - 1)
                    transpose_probs(pt[t % 2], p_sb[:, (t - LAG_T) % 4, :])
                if live(first, t, LAG_V):
                    u = (t - LAG_V) % (2 * TP)
                    pe.wait_ge(p_ready, n - LAG_V + 1)
                    if u % TP == 0:
                        pe.wait_ge(v_ready, g + (t - LAG_V) // TP + 1)
                        if not (first and t == LAG_V):
                            pe.wait_ge(o_ready, g + (t - LAG_V) // TP)
                    weigh_values(u % TP // NT, u % NT, u % 4, u // TP)
                if t < 2 * TP:
                    if t % TP == 0:
                        pe.wait_ge(qk_ready, (g + t // TP) * 2 + 2)
                    if not (first and t < 2):
                        pe.wait_ge(probs_ready, n - 1)
                    scores(sc[t % 2], t % TP // NT, t % NT)
                    if t % TP == 1:
                        project_v("cross", t // TP)
                if after_pair(first, t, LAG_V) is not None:
                    q = after_pair(first, t, LAG_V)
                    pe.wait_ge(o_ready, g + q + 1)
                    turn_outputs()
                if t < 2 * TP and t % TP == TP - 2 and not (last and t > TP):
                    pe.wait_ge(v_rest_ready, g + t // TP + 1)
                    project_qk("cross", g + t // TP + 1, (t // TP + 1) % 2, None if first and t < TP else g + t // TP)

            def project_out(kind, phase):
                pe.wait_ge(ot_copied, (phase + 1) * PAIRS)
                for i in range(NT):
                    acc = sc[i // 2][:, (i % 2) * D:(i % 2 + 1) * D]
                    nc.tensor.matmul(acc, ones_row[:], bo[kind][:], start=True, stop=False)
                    for p in range(PAIRS):
                        last = nc.tensor.matmul(acc, o_T[:, p, i * P:(i + 1) * P], wo[kind][:, p, :],
                                                start=False, stop=(p == PAIRS - 1))
                last.then_inc(acc_ready, 1)

            def turn_rows(phase, rows):
                pe.wait_ge(norm_ready, (phase + 1) * NT)
                for c in range(DC):
                    for i in range(NT):
                        last = nc.tensor.transpose(pt[c][:, i * P:(i + 1) * P], rows[:, i, c * P:(c + 1) * P], ident[:])
                last.then_inc(nt_ready, 1)

            pe.wait_ge(ident_set, 2)
            pe.wait_ge(consts_set, 5)
            pe.wait_ge(const_loaded, 5 * 16)
            with pe.Fori(0, B) as b:
                pe.wait_ge(x_loaded, 16 * b + 16)
                self_attention(pe, b, period)
                project_out("self", 2 * b)
                turn_rows(2 * b, x1)
                pe.wait_ge(ctx_loaded, 32 * b + 32)
                pe.wait_ge(nt_copied, (2 * b + 1) * DC)
                cross_attention(pe, b, slot)
                project_out("cross", 2 * b + 1)
                turn_rows(2 * b + 1, x2_now)
            pe.wait_ge(nt_copied, 2 * B * DC)
            for i in range(NU):
                for c in range(DC):
                    last = nc.tensor.matmul(logits[:, i, :], x2_T[:, c, i, :], gw[:, c, :], start=(c == 0), stop=(c == DC - 1))
            last.then_inc(logits_ready, 1)

            gate_up, turned, down = sc, pt, proj
            with pe.Fori(0, E // 2) as ep:
                for j in range(2 * NU + 2):
                    n = ep * (2 * NU) + j
                    if j < 2 * NU:
                        k, i = j // NU, j % NU
                        if i == 0:
                            pe.wait_ge(experts_loaded[k], ep * 32 + 32)
                        if j >= 2:
                            pe.wait_ge(act_ready, n - 1)
                        for c in range(DC):
                            last = nc.tensor.matmul(gate_up[j % 2][:], x2_T[:, c, i, :], w_gu[:, k, c, :],
                                                    start=(c == 0), stop=(c == DC - 1))
                        last.then_inc(gu_ready, 1)
                    if 0 <= j - 1 < 2 * NU:
                        pe.wait_ge(act_ready, n)
                        if j - 1 >= 2:
                            pe.wait_ge(at_copied, n - 2)
                        for c in range(FC):
                            last = nc.tensor.transpose(turned[(j - 1) % 2][:, c * P:(c + 1) * P],
                                                       act_sb[:, (j - 1) % 2, c * P:(c + 1) * P], ident[:])
                        last.then_inc(at_ready, 1)
                    if 0 <= j - 2 < 2 * NU:
                        k = (j - 2) // NU
                        pe.wait_ge(at_copied, n - 1)
                        if j - 2 >= 2:
                            pe.wait_ge(moe_added, n - 3)
                        for c in range(FC):
                            last = nc.tensor.matmul(down[j % 2][:, 0:D], act_T[:, j % 2, c * P:(c + 1) * P],
                                                    w_dn[:, k, c, :], start=(c == 0), stop=(c == FC - 1))
                        last.then_inc(down_ready, 1)

        @block.scalar
        def _(act):
            def copy_qk(kind, g, fresh):
                act.wait_ge(q_proj, g + 1)
                if not fresh:
                    act.wait_ge(scores_ready, g * TP)
                nc.scalar.copy(q_high[:], proj[0][:]).then_inc(q_high_ready, 1)
                act.wait_ge(k_proj, g + 1)
                nc.scalar.mul(k_high[:], proj[1][:], SCALE[kind]).then_inc(k_high_ready, 1)

            def copy_v(g, fresh):
                act.wait_ge(v_proj, g + 1)
                if not fresh:
                    act.wait_ge(v_rest_ready, g)
                nc.scalar.activation(v_sb[:], proj[0][:], ACT.Relu).then_inc(v_copied, 1)

            def copy_outputs(gn, p):
                act.wait_ge(ot_ready, gn)
                nc.scalar.mul(o_T[:, p, :], proj[1][:], 1.0 / P_SCALE).then_inc(ot_copied, 1)

            def period(first, last, nb, ns, gg, g, gs, r, j):
                def tile(lag, i):
                    return (j - lag) * GT + i

                def copy_scores(i):
                    act.wait_ge(scores_ready, nb + tile(0, i) + 1)
                    if not first:
                        act.wait_ge(probs_ready, nb + tile(4, i) + 1)
                    nc.scalar.activation(s_sb[:, j, i, :], sc[i % 2][:], ACT.Copy,
                                         accum_out=s_sum[:, j, i:i + 1]).then_inc(scores_copied, 1)

                def count(c, i):
                    jj = (j - 1) % RING
                    act.wait_ge(cut_ready[c], gg + j)
                    if c < 2:
                        ins = nc.scalar.activation(side_unused[:, i, :], s_sb[:, jj, i, :], ACT.Sign, bias=neg_cut[:, jj, c, i:i + 1],
                                                   scale=1.0, accum_out=sides[:, jj, c, i:i + 1])
                    else:
                        if not (first and j < 3):
                            act.wait_ge(below_step, 4 * (ns + tile(3, 0) + GT))
                        ins = nc.scalar.activation(side[:, jj % 2, i, :], s_sb[:, jj, i, :], ACT.Sign,
                                                   bias=neg_cut[:, jj, c, i:i + 1], scale=1.0, accum_out=sides[:, jj, c, i:i + 1])
                    ins.then_inc(sides_ready[c], 1)

                def exponential(i):
                    jj = (j - 3) % RING
                    if not (first and j == 3):
                        act.wait_ge(probs_ready, nb + tile(4, i) + 1)
                    nc.scalar.activation(e_sb[:, i, :], s_sb[:, jj, i, :], ACT.Exp, bias=neg_top[:, jj, i:i + 1],
                                         scale=1.0).then_inc(exp_ready, 1)

                def copy_turned(i):
                    act.wait_ge(pt_ready, nb + tile(3, i) + 1)
                    if not (first and j == 3 and i < 2):
                        act.wait_ge(p_ready, nb + tile(3, i) - 1)
                    nc.scalar.mul(p_T[:, i % 2, :], pt[i % 2][:], P_SCALE).then_inc(pt_copied, 1)

                new, cuts, old = due(first, j, 0), due(first, j, 1), due(first, j, 3)
                if first and j == 0:
                    copy_qk("self", g, True)
                if old:
                    exponential(0)
                    exponential(1)
                if new:
                    copy_scores(0)
                    copy_scores(1)
                if old:
                    exponential(2)
                    exponential(3)
                if cuts:
                    for i in range(GT):
                        count(0, i)
                if new:
                    copy_scores(2)
                    copy_scores(3)
                    if j % 2 == 1:
                        copy_v(g + j // 2, first and j == 1)
                if old:
                    copy_turned(0)
                    copy_turned(1)
                if cuts:
                    for i in range(GT):
                        count(1, i)
                if old:
                    copy_turned(2)
                    copy_turned(3)
                if j % 2 == 1 and due(first, j - 1, 4):
                    copy_outputs(g + (j - 3) // 2, r * 2 + (j - 5) // 2)
                if cuts:
                    for i in range(GT):
                        count(2, i)
                if new and j % 2 == 1 and not (last and j == RING - 1):
                    copy_qk("self", g + j // 2 + 1, False)

            def slot(first, last, g, nx, r, t):
                n = g * TP + t
                if first and t == 0:
                    copy_qk("cross", g, True)
                if live(first, t, 1):
                    u = (t - 1) % (2 * TP)
                    act.wait_ge(max_ready, nx + t)
                    if not (first and t - 1 < 4):
                        act.wait_ge(pt_ready, n - 4)
                    if t % TP == 1 and not (first and t == 1):
                        act.wait_ge(inv_ready, g + t // TP)
                    at = 2 * (u % NT) + u % TP // NT
                    nc.scalar.activation(p_sb[:, u % 4, :], sc[u % 2][:], ACT.Exp,
                                         bias=neg_max[:, u % 4:u % 4 + 1], scale=1.0,
                                         accum_out=row_sum[:, at:at + 1]).then_inc(probs_ready, 1)
                if live(first, t, LAG_T):
                    act.wait_ge(pt_ready, n - LAG_T + 1)
                    if not (first and t - LAG_T < 4):
                        act.wait_ge(pv_done, n - LAG_T - 3)
                    nc.scalar.mul(p_high[:, (t - LAG_T) % 4, :], pt[t % 2][:], P_SCALE).then_inc(p_high_ready, 1)
                if t < 2 * TP and t % TP == 2:
                    act.wait_ge(v_proj, g + t // TP + 1)
                    nc.scalar.copy(v_part[:, t // TP, 0].rearrange("p c d -> p (c d)"), proj[0][:]).then_inc(v_copied, 1)
                q = after_pair(first, t, LAG_V + 1)
                if q is not None:
                    copy_outputs(g + q + 1, r * 2 + q)
                if t < 2 * TP and t % TP == TP - 1 and not (last and t > TP):
                    copy_qk("cross", g + t // TP + 1, False)

            with act.Fori(0, B) as b:
                self_attention(act, b, period)
                act.wait_ge(nt_ready, 2 * b + 1)
                for c in range(DC):
                    nc.scalar.copy(x1_T[:, c, :], pt[c][:]).then_inc(nt_copied, 1)
                cross_attention(act, b, slot)
                act.wait_ge(nt_ready, 2 * b + 2)
                for c in range(DC):
                    nc.scalar.copy(x2_T[:, c, bass.ds(b * NT, NT), :].rearrange("p n t -> p (n t)"), pt[c][:]).then_inc(nt_copied, 1)
            act.wait_ge(centred, 1)
            nc.scalar.activation(probs[:], route[:], ACT.Exp).then_inc(rexp_ready, 1)
            with act.Fori(0, E // 2) as ep:
                for j in range(2 * NU + 1):
                    n = ep * (2 * NU) + j
                    if j < 2 * NU:
                        act.wait_ge(gu_ready, n + 1)
                        if j >= 2:
                            act.wait_ge(hid_ready, n - 1)
                        nc.scalar.activation(th[:, j % 2, :], sc[j % 2][:, 0:F], ACT.Tanh, scale=0.5).then_inc(th_ready, 1)
                    if j >= 1:
                        act.wait_ge(at_ready, n)
                        if j - 1 >= 2:
                            act.wait_ge(down_ready, n - 2)
                        nc.scalar.copy(act_T[:, (j - 1) % 2, :], pt[(j - 1) % 2][:, 0:F]).then_inc(at_copied, 1)

        @block.vector
        def _(dve):
            def exact_search(jj, i):
                scores = s_sb[:, jj, i, :]
                for q in range(ROUNDS):
                    dve.drain()
                    nc.vector.max(best[:, q, :], scores)
                    dve.drain()
                    if q < ROUNDS - 1:
                        nc.vector.match_replace(exact[:, q % 2, :], best[:, q, :], scores, TAKEN)
                        scores = exact[:, q % 2, :]
                nc.vector.tensor_copy(found[:, jj, 1, i:i + 1], best[:, ROUNDS - 1, KTH:KTH + 1])
                dve.drain()

            def low_parts(kind, g):
                dve.wait_ge(q_high_ready, g + 1)
                nc.vector.tensor_tensor(q_low[:], proj[0][:], q_high[:].bitcast(F32), ALU.subtract).then_inc(qk_ready, 1)
                dve.wait_ge(k_high_ready, g + 1)
                nc.vector.scalar_tensor_tensor(out=k_low[:], in0=proj[1][:], scalar=SCALE[kind], in1=k_high[:].bitcast(F32),
                                               op0=ALU.mult, op1=ALU.subtract).then_inc(qk_ready, 1)

            def invert_sums(gn):
                dve.wait_ge(probs_ready, gn * TP)
                nc.vector.reciprocal(row_inv[:], row_sum[:]).then_inc(inv_ready, 1)

            def normalize(gn):
                dve.wait_ge(pv_done, gn * TP)
                dve.wait_ge(inv_ready, gn)
                nc.vector.tensor_tensor(o_sb[:], o_ps[:], row_inv[:].rearrange("p (n o) -> p n o", o=1).to_broadcast([P, TP, DH]),
                                        ALU.mult).then_inc(o_ready, 1)

            def period(first, last, nb, ns, gg, g, gs, r, j):
                def tile(lag, i):
                    return (j - lag) * GT + i

                def top(i):
                    stand_alone(dve, scores_copied, ns + tile(0, i) + 1)
                    nc.vector.max(top8[:, j, i, :], s_sb[:, j, i, :]).then_inc(top_ready, 1)

                def next_below(i0):
                    jj = (j - 2) % RING
                    step = 4 * (ns + tile(2, i0))
                    for i in (i0, i0 + 1):
                        dve.wait_ge(sides_ready[2], ns + tile(2, i) + 1)
                        nc.vector.scalar_tensor_tensor(out=below[:, i % 2, :], in0=side[:, jj % 2, i, :], scalar=-CUT,
                                                       in1=s_sb[:, jj, i, :], op0=ALU.mult, op1=ALU.min,
                                                       accum_out=cut_sum[:, jj, i:i + 1]).then_inc(below_step, 1)
                    for i in (i0, i0 + 1):
                        stand_alone(dve, below_step, step + 1 + i % 2)
                        nc.vector.max(next16[:, i, 0:8], below[:, i % 2, :]).then_inc(below_step, 1)
                    for i in (i0, i0 + 1):
                        stand_alone(dve, below_step, step + 3 + i % 2)
                        nc.vector.match_replace(below2[:, i % 2, :], next16[:, i, 0:8], below[:, i % 2, :], TAKEN).then_inc(below_step, 1)
                    for i in (i0, i0 + 1):
                        stand_alone(dve, below_step, step + 5 + i % 2)
                        nc.vector.max(next16[:, i, 8:16], below2[:, i % 2, :]).then_inc(below_step, 1)

                def pick():
                    n, jj = gg + (j - 2), (j - 2) % RING
                    dve.wait_ge(below_step, 4 * (ns + tile(2, 0) + GT))
                    nc.vector.tensor_scalar(place[:], cut_sum[:, jj, :], 1.0 / CUT, float(K_TOP - 1), ALU.mult, ALU.add).then_inc(pick_step, 1)
                    dve.wait_ge(pick_step, 3 * n + 1)
                    nc.vector.tensor_tensor(picked[:, 0], places[:], place[:].rearrange("p (n o) -> p n o", o=1).to_broadcast([P, GT, WINDOW]),
                                            ALU.is_equal).then_inc(pick_step, 1)
                    dve.wait_ge(pick_step, 3 * n + 2)
                    nc.vector.tensor_tensor(picked[:, 1], picked[:, 0], next16[:], ALU.mult).then_inc(pick_step, 1)
                    dve.wait_ge(pick_step, 3 * n + 3)
                    nc.vector.tensor_reduce(found[:, jj], picked[:], AX.X, ALU.add).then_inc(found_ready, 1)

                def check():
                    n, jj = gg + (j - 3), (j - 3) % RING
                    dve.wait_ge(ok_summed, n + 1)
                    dve.wait_ge(found_ready, n + 1)
                    nc.vector.tensor_copy(rows_ok[0:1, 0:GT], ok_ps).then_inc(ok_read, 1)
                    nc.vector.tensor_reduce(rows_ok[0:1, GT:GT + 1], ok_ps, AX.X, ALU.min).then_inc(ok_read, 1)
                    stand_alone(dve, ok_read, 2 * n + 2)
                    least = dve.value_load(rows_ok[0:1, GT:GT + 1], min_val=0, max_val=P)
                    with dve.If(least < P):
                        for i in range(GT):
                            rows = dve.value_load(rows_ok[0:1, i:i + 1], min_val=0, max_val=P)
                            with dve.If(rows < P):
                                exact_search(jj, i)

                def mask(i):
                    jj = (j - 3) % RING
                    at = 2 * i + jj % 2
                    dve.wait_ge(exp_ready, ns + tile(3, i) + 1)
                    if not (first and j == 3):
                        dve.wait_ge(pt_ready, nb + tile(4, i) + 1)
                    nc.vector.scalar_tensor_tensor(out=p_sb[:, i, :], in0=s_sb[:, jj, i, :], scalar=found[:, jj, 1, i:i + 1],
                                                   in1=e_sb[:, i, :], op0=ALU.is_ge, op1=ALU.mult,
                                                   accum_out=row_sum[:, at:at + 1]).then_inc(probs_ready, 1)

                new, low, old = due(first, j, 0), due(first, j, 2), due(first, j, 3)
                ended = j % 2 == 1 and due(first, j - 1, 4)
                if first and j == 0:
                    low_parts("self", g)
                if ended:
                    invert_sums(g + (j - 3) // 2)
                if old:
                    check()
                    mask(0)
                    mask(1)
                if new:
                    top(0)
                    top(1)
                if low:
                    next_below(0)
                if ended:
                    normalize(g + (j - 3) // 2)
                if old:
                    mask(2)
                    mask(3)
                if low:
                    next_below(2)
                    pick()
                if new:
                    top(2)
                    top(3)
                if new and j % 2 == 1 and not (last and j == RING - 1):
                    low_parts("self", g + j // 2 + 1)

            def slot(first, last, g, nx, r, t):
                n = g * TP + t
                if first and t == 0:
                    low_parts("cross", g)
                if live(first, t, LAG_T):
                    k = (t - LAG_T) % 4
                    dve.wait_ge(p_high_ready, n - LAG_T + 1)
                    nc.vector.scalar_tensor_tensor(out=p_low[:, k, :], in0=pt[t % 2][:], scalar=P_SCALE, in1=p_high[:, k, :],
                                                   op0=ALU.mult, op1=ALU.subtract).then_inc(p_ready, 1)
                if t < 2 * TP:
                    dve.wait_ge(scores_ready, n + 1)
                    nc.vector.tensor_reduce(neg_max[:, t % 4:t % 4 + 1], sc[t % 2][:], AX.X, ALU.max, negate=True).then_inc(max_ready, 1)
                if t < 2 * TP and t % TP == 2:
                    dve.wait_ge(v_copied, g + t // TP + 1)
                    if not (first and t == 2):
                        dve.wait_ge(v_ready, g + t // TP)
                    nc.vector.tensor_tensor(v_rest[:], proj[0][:], v_part[:, t // TP, 0].rearrange("p c d -> p (c d)"),
                                            ALU.subtract).then_inc(v_rest_ready, 1)
                q = after_pair(first, t, 0)
                if q is not None:
                    invert_sums(g + q + 1)
                q = after_pair(first, t, LAG_V - 1)
                if q is not None:
                    normalize(g + q + 1)
                if t < 2 * TP and t % TP == TP - 1 and not (last and t > TP):
                    low_parts("cross", g + t // TP + 1)

            NSTEP = 2 + NT + NT

            def norm(m, add, dst):
                rows = add()
                dve.wait_ge(norm_step, m * NSTEP + 2)
                for i in range(NT):
                    nc.vector.bn_stats(stats[:, i, :], rows(i)).then_inc(norm_step, 1)
                for i in range(NT):
                    stand_alone(dve, norm_step, m * NSTEP + 2 + i + 1)
                    nc.vector.bn_aggr(mean_var[:, i, :], stats[:, i, :]).then_inc(norm_step, 1)
                dve.wait_ge(norm_step, m * NSTEP + NSTEP)
                nc.vector.tensor_scalar(var_eps[:], mean_var[:, :, 1], LN_EPS, None, ALU.add).then_inc(vare_ready, 1)
                dve.wait_ge(rstd_ready, m + 1)
                for i in range(NT):
                    nc.vector.tensor_scalar(dst(i), rows(i), mean_var[:, i, 0:1], rstd[:, i:i + 1],
                                            ALU.subtract, ALU.mult).then_inc(norm_ready, 1)

            def norm_attention(phase, res, dst):
                def add():
                    dve.wait_ge(acc_ready, phase + 1)
                    for j in range(2):
                        nc.vector.tensor_tensor(y_sb[:, 2 * j:2 * j + 2, :].rearrange("p n d -> p (n d)"), sc[j][:],
                                                res[:, 2 * j:2 * j + 2, :].rearrange("p n d -> p (n d)"), ALU.add).then_inc(norm_step, 1)
                    return lambda i: y_sb[:, i, :]
                norm(phase, add, lambda i: dst[:, i, :])

            with dve.Fori(0, B) as b:
                self_attention(dve, b, period)
                dve.wait_ge(res_loaded, 16 * b + 16)
                norm_attention(2 * b, x1, x1)
                cross_attention(dve, b, slot)
                norm_attention(2 * b + 1, x1, x2_now)

            steps = [0]

            def step(ins):
                ins.then_inc(route_step, 1)
                steps[0] += 1
                dve.wait_ge(route_step, steps[0])

            def wide(c):
                return c.rearrange("p (n o) -> p n o", o=1).to_broadcast([P, NU, E])

            dve.wait_ge(logits_ready, 1)
            step(nc.vector.tensor_reduce(col[:, 0, :], logits[:], AX.X, ALU.max))
            nc.vector.tensor_tensor(route[:], logits[:], wide(col[:, 0, :]), ALU.subtract).then_inc(centred, 1)
            dve.wait_ge(rexp_ready, 1)
            step(nc.vector.tensor_reduce(col[:, 1, :], probs[:], AX.X, ALU.add))
            step(nc.vector.reciprocal(col[:, 2, :], col[:, 1, :]))
            step(nc.vector.tensor_tensor(probs[:], probs[:], wide(col[:, 2, :]), ALU.mult))
            for i in range(NU):
                last = nc.vector.max(r_top[:, i, :], probs[:, i, :])
            step(last)
            second = r_top[:, :, TOP_EXPERTS - 1]
            step(nc.vector.tensor_copy(col[:, 3, :], second))
            step(nc.vector.tensor_tensor(above[:], probs[:], wide(col[:, 3, :]), ALU.is_gt))
            step(nc.vector.tensor_tensor(equal[:], probs[:], wide(col[:, 3, :]), ALU.is_equal))
            step(nc.vector.tensor_copy(rank[:, 0], equal[:]))
            shift, a = 1, 0
            while shift < E:
                step(nc.vector.tensor_copy(rank[:, (a + 1) % 3, :, 0:shift], rank[:, a, :, 0:shift]))
                step(nc.vector.tensor_tensor(rank[:, (a + 1) % 3, :, shift:E], rank[:, a, :, shift:E],
                                             rank[:, a, :, 0:E - shift], ALU.add))
                shift, a = 2 * shift, (a + 1) % 3
            step(nc.vector.tensor_reduce(col[:, 4, :], above[:], AX.X, ALU.add))
            step(nc.vector.tensor_scalar(col[:, 5, :], col[:, 4, :], -1.0, float(TOP_EXPERTS), ALU.mult, ALU.add))
            step(nc.vector.tensor_tensor(rank[:, a], rank[:, a], wide(col[:, 5, :]), ALU.is_le))
            step(nc.vector.tensor_tensor(equal[:], equal[:], rank[:, a], ALU.mult))
            step(nc.vector.tensor_tensor(above[:], above[:], equal[:], ALU.add))
            step(nc.vector.tensor_tensor(route[:], probs[:], above[:], ALU.mult))
            for again in range(2):
                step(nc.vector.tensor_reduce(col[:, 6, :], route[:], AX.X, ALU.add))
                step(nc.vector.tensor_scalar(col[:, 6, :], col[:, 6, :], ROUTE_EPS, None, ALU.add))
                step(nc.vector.reciprocal(col[:, 7, :], col[:, 6, :]))
                step(nc.vector.tensor_tensor(route[:], route[:], wide(col[:, 7, :]), ALU.mult))
            step(nc.vector.tensor_scalar(route[:], route[:], 0.5, None, ALU.mult))

            dve.wait_ge(moe_started, B)
            with dve.Fori(0, E // 2) as ep:
                for j in range(2 * NU + 2):
                    n = ep * (2 * NU) + j
                    if j < 2 * NU:
                        dve.wait_ge(th_ready, n + 1)
                        nc.vector.scalar_tensor_tensor(out=hid[:, j % 2, :], in0=th[:, j % 2, :], scalar=1.0,
                                                       in1=sc[j % 2][:, 0:F], op0=ALU.add, op1=ALU.mult).then_inc(hid_ready, 1)
                        dve.wait_ge(hid_ready, n + 1)
                        if j >= 2:
                            dve.wait_ge(at_ready, n - 1)
                        nc.vector.tensor_tensor(act_sb[:, j % 2, :], hid[:, j % 2, :], sc[j % 2][:, F:2 * F], ALU.mult).then_inc(act_ready, 1)
                    if j >= 2:
                        k, i = (j - 2) // NU, (j - 2) % NU
                        dve.wait_ge(down_ready, n - 1)
                        nc.vector.scalar_tensor_tensor(out=moe[:, i, :], in0=proj[j % 2][:, 0:D],
                                                       scalar=route[:, i, bass.ds(ep * 2 + k, 1)], in1=moe[:, i, :],
                                                       op0=ALU.mult, op1=ALU.add).then_inc(moe_added, 1)
            dve.wait_ge(moe_added, E * NU)
            with dve.Fori(0, B) as b:
                def whole():
                    dve.wait_ge(norm_ready, (2 * B + b) * NT)
                    nc.vector.tensor_copy(y_sb[:, 0:2, :], moe[:, bass.ds(b * NT, 2), :]).then_inc(norm_step, 1)
                    nc.vector.tensor_copy(y_sb[:, 2:4, :], moe[:, bass.ds(b * NT + 2, 2), :]).then_inc(norm_step, 1)
                    return lambda i: y_sb[:, i, :]
                norm(2 * B + b, whole, lambda i: moe[:, bass.ds(b * NT + i, 1), :].rearrange("p n d -> p (n d)"))


def kernel(x, ctx_768, L0_attn_W_qkv, L0_attn_W_out, L0_attn_b_out, L0_xattn_w_q, L0_xattn_w_k, L0_xattn_w_v,
           L0_xattn_w_o, L0_xattn_b_o, L0_ffn_gate_w, L0_ffn_gate_up_proj, L0_ffn_down_proj):
    import numpy as np
    import concourse.bacc as bacc
    from concourse.bass_utils import run_bass_kernel_spmd

    x, ctx_768 = np.asarray(x), np.asarray(ctx_768)
    B, T, D = x.shape
    CTX = ctx_768.shape[2]
    INNER = L0_xattn_w_q.shape[1]
    PAIRS = INNER // P

    def pair_weights(q, k, v):
        w = np.zeros((PAIRS, P, 3, 2, P), np.float32)
        for n, m in enumerate((q, k, v)):
            for c in range(2):
                rows = np.asarray(m)[c * P:(c + 1) * P]
                w[:, :rows.shape[0], n, c, :] = rows.reshape(rows.shape[0], PAIRS, P).transpose(1, 0, 2)
        return w

    qkv = np.asarray(L0_attn_W_qkv).T
    arrays = {
        "xT": x.transpose(0, 2, 1).reshape(B, D // P, P, T),
        "x": x,
        "ctxT": ctx_768.transpose(0, 2, 1),
        "w_self": pair_weights(qkv[:, :INNER], qkv[:, INNER:2 * INNER], qkv[:, 2 * INNER:]),
        "wo_self": np.asarray(L0_attn_W_out).T.reshape(PAIRS, P, D).transpose(1, 0, 2),
        "bo_self": np.asarray(L0_attn_b_out).reshape(1, D),
        "w_cross": pair_weights(L0_xattn_w_q, L0_xattn_w_k, L0_xattn_w_v),
        "wo_cross": np.asarray(L0_xattn_w_o).reshape(PAIRS, P, D).transpose(1, 0, 2),
        "bo_cross": np.asarray(L0_xattn_b_o).reshape(1, D),
        "gate_wT": np.asarray(L0_ffn_gate_w).T.reshape(D // P, P, -1).transpose(1, 0, 2),
    }
    gu, dn = np.asarray(L0_ffn_gate_up_proj), np.asarray(L0_ffn_down_proj)
    arrays["w_gate_up"] = gu.reshape(gu.shape[0], D // P, P, -1).transpose(0, 2, 1, 3)
    arrays["w_down"] = dn.reshape(dn.shape[0], dn.shape[1] // P, P, D).transpose(0, 2, 1, 3)
    arrays = {n: np.ascontiguousarray(a) for n, a in arrays.items()}
    nc = bacc.Bacc("TRN2", target_bir_lowering=False, num_devices=1)
    args = [nc.dram_tensor(n, a.shape, mybir.dt.from_np(a.dtype), kind="ExternalInput").ap() for n, a in arrays.items()]
    args.append(nc.dram_tensor("out", x.shape, F32, kind="ExternalOutput").ap())
    decoder_kernel(nc, *args)
    r = run_bass_kernel_spmd(nc, [arrays], core_ids=[0])
    return r.results[0]["out"]
```

```python
from contextlib import ExitStack

import concourse.bass as bass
from concourse import mybir

F32 = mybir.dt.float32
BF16 = mybir.dt.bfloat16
F16 = mybir.dt.float16
F32R = mybir.dt.float32r
I32 = mybir.dt.int32
ALU = mybir.AluOpType
ACT = mybir.ActivationFunctionType
AX = mybir.AxisListType

P = 128
TAKEN = -3.0e38
CUT = 2.0 ** 100
LN_EPS = 1e-5
ROUTE_EPS = 1e-9
TOP_EXPERTS = 2


def decoder_kernel(nc, xT, x, ctxT, w_self, wo_self, bo_self, w_cross, wo_cross, bo_cross,
                   gate_wT, w_gate_up, w_down, out):
    B, DC, _, T = xT.shape
    D = x.shape[2]
    PAIRS = w_self.shape[0]
    DH = P // 2
    E = w_gate_up.shape[0]
    FC = w_down.shape[2]
    F = FC * P
    NT = T // P
    TP = 2 * NT
    CTX = ctxT.shape[1]
    CTX1 = CTX - P
    NU = B * NT
    K_TOP = max(1, int(0.1 * T))
    ROUNDS = (K_TOP + 7) // 8
    SPLIT_AT = 4
    KTH = (K_TOP - 1) % 8
    GT = NT
    RING = 4
    LOOPS = 2 * PAIRS // RING
    WINDOW = 16
    MIDDLE = K_TOP - WINDOW / 2 - 0.5
    FIRST_CUT = 0.6
    SLOPE = 0.9 * T / 512 / (2.2193 * 80)
    MOVES = ((1.15 * SLOPE, MIDDLE + 2.5), (0.65 * SLOPE, MIDDLE))
    P_SCALE = 2.0 ** 12
    SCALE = {"self": float(D) ** -0.5, "cross": float(DH) ** -0.5}

    with ExitStack() as ctx:
        def sb(name, shape, dt=F32):
            return ctx.enter_context(nc.sbuf_tensor(name, shape, dt))

        def psum(name, shape):
            return ctx.enter_context(nc.psum_tensor(name, shape, F32))

        def sem(name):
            return ctx.enter_context(nc.semaphore(name))

        ident = sb("ident", [P, P])
        ones_row = sb("ones_row", [1, P])
        neg_half = sb("neg_half", [P, NU])
        bo = {"self": sb("bo_s", [1, D]), "cross": sb("bo_c", [1, D])}
        wo = {"self": sb("wo_s", [P, PAIRS, D]), "cross": sb("wo_c", [P, PAIRS, D])}
        gw = sb("gw", [P, DC, E])
        x_T = sb("x_T", [P, DC, T])
        ctx_T0 = sb("ctx_T0", [P, T])
        ctx_T1 = sb("ctx_T1", [CTX1, T])
        x1 = sb("x1", [P, NT, D])
        w_pair = sb("w_pair", [P, 2, 3, 2, P])
        q_high, q_low = sb("q_high", [P, 2, T], F32R), sb("q_low", [P, 2, T], F32R)
        k_high, k_low = sb("k_high", [P, 2, T], F32R), sb("k_low", [P, 2, T], F32R)
        v_sb = sb("v_sb", [P, T])
        v_rest = sb("v_rest", [P, T])
        v_part = sb("v_part", [P, 2, 3, NT, P], BF16)
        neg_max = sb("neg_max", [P, 4])
        s_sb = sb("s_sb", [P, RING, GT, T])
        top8 = sb("top8", [P, RING, GT, 8])
        s_sum = sb("s_sum", [P, RING, GT])
        spread = sb("spread", [P, RING, GT])
        neg_cut = sb("neg_cut", [P, RING, 3, GT])
        sides = sb("sides", [P, RING, 3, GT])
        neg_top = sb("neg_top", [P, RING, GT])
        p_tmp = sb("p_tmp", [P, 6, GT])
        side = sb("side", [P, 2, GT, T], BF16)
        below = sb("below", [P, 2, T])
        below2 = sb("below2", [P, 2, T])
        cut_sum = sb("cut_sum", [P, RING, GT])
        next16 = sb("next16", [P, GT, WINDOW])
        place = sb("place", [P, GT])
        picked = sb("picked", [P, 2, GT, WINDOW])
        found = sb("found", [P, RING, 2, GT])
        places_i = sb("places_i", [P, GT, WINDOW], I32)
        places = sb("places", [P, GT, WINDOW])
        ones_col = sb("ones_col", [P, 1])
        row_ok = sb("row_ok", [P, GT])
        rows_ok = sb("rows_ok", [1, 8], I32)
        best = sb("best", [P, ROUNDS, 8])
        row_sum = sb("row_sum", [P, TP])
        row_inv = sb("row_inv", [P, TP])
        e_sb = sb("e_sb", [P, GT, T])
        x2_now = e_sb[:].rearrange("p i t -> p (i t)")[:, 0:NT * D].rearrange("p (n d) -> p n d", n=NT)
        p_sb = sb("p_sb", [P, 4, T])
        p_T = sb("p_T", [P, 2, T])
        p_high, p_low = sb("p_high", [P, 4, T], F16), sb("p_low", [P, 4, T], F16)
        o_sb = sb("o_sb", [P, TP, DH])
        o_T = sb("o_T", [P, PAIRS, T])
        y_sb = sb("y_sb", [P, NT, D])
        exact = y_sb[:].rearrange("p (a n) d -> p a (n d)", a=2)
        stats = sb("stats", [P, NT, 6])
        mean_var = sb("mean_var", [P, NT, 2])
        var_eps = sb("var_eps", [P, NT])
        rstd = sb("rstd", [P, NT])
        moe = sb("moe", [P, NU, D])
        x2_T = sb("x2_T", [P, DC, NU, P])
        s_flat = s_sb[:].rearrange("p k i t -> p (k i t)")
        w_gu = s_flat[:, 0:4 * DC * F].rearrange("p (k c f) -> p k c f", k=2, c=DC)
        w_dn = s_flat[:, 4 * DC * F:4 * DC * F + 2 * FC * D].rearrange("p (k c d) -> p k c d", k=2, c=FC)
        gu_high = [part[:, :, 0:2 * F] for part in (q_high, k_high)]
        gu_low = [part[:, :, 0:2 * F] for part in (q_low, k_low)]
        row_high, row_low = sb("row_high", [P, 2, DC, P], F32R), sb("row_low", [P, 2, DC, P], F32R)
        rank_at = 4 * DC * F + 2 * FC * D + 4 * F
        rank = s_flat[:, rank_at:rank_at + 3 * NU * E].rearrange("p (k n e) -> p k n e", k=3, n=NU)
        last_at = rank_at + 3 * NU * E
        last_stats = s_flat[:, last_at:last_at + 6 * NU].rearrange("p (n k) -> p n k", n=NU)
        last_mean_var = s_flat[:, last_at + 6 * NU:last_at + 8 * NU].rearrange("p (n k) -> p n k", n=NU)
        last_var_eps = s_flat[:, last_at + 8 * NU:last_at + 9 * NU]
        last_rstd = s_flat[:, last_at + 9 * NU:last_at + 10 * NU]
        probs = sb("probs", [P, NU, E])
        above = sb("above", [P, NU, E])
        equal = sb("equal", [P, NU, E])
        r_top = sb("r_top", [P, NU, 8])
        col = sb("col", [P, 8, NU])
        route = sb("route", [P, NU, E])
        th_hid = sb("th_hid", [P, 2, 2, F])
        th, hid = th_hid[:, 0], th_hid[:, 1]
        side_unused = th_hid[:].rearrange("p a b f -> p (a b f)").bitcast(BF16).rearrange("p (i t) -> p i t", i=GT)
        act_at = 4 * DC * F + 2 * FC * D
        act_sb = s_flat[:, act_at:act_at + 2 * F].rearrange("p (k f) -> p k f", k=2)
        act_T = s_flat[:, act_at + 2 * F:act_at + 4 * F].rearrange("p (k f) -> p k f", k=2)

        proj = [psum("proj0", [P, T]), psum("proj1", [P, T])]
        sc = [psum("sc0", [P, T]), psum("sc1", [P, T])]
        pt = [psum("pt0", [P, T]), psum("pt1", [P, T])]
        o_ps = psum("o_ps", [P, TP, DH])
        spare = psum("spare", [P, TP, DH])
        spare_flat = spare[:].rearrange("p n d -> p (n d)")
        outputs = [o_ps, spare]
        ok_ps = spare_flat[0:1, 0:GT]
        logits = spare_flat[:, 0:NU * E].rearrange("p (n e) -> p n e", n=NU)

        const_loaded, ident_set, consts_set = sem("const_loaded"), sem("ident_set"), sem("consts_set")
        x_loaded, ctx_loaded, res_loaded = sem("x_loaded"), sem("ctx_loaded"), sem("res_loaded")
        w_loaded = [sem("w_even_loaded"), sem("w_odd_loaded")]
        q_proj, k_proj, q_high_ready, k_high_ready, qk_ready = (
            sem("q_proj"), sem("k_proj"), sem("q_high_ready"), sem("k_high_ready"), sem("qk_ready"))
        v_proj, v_copied, v_first, v_rest_ready, v_second, v_ready = (
            sem("v_proj"), sem("v_copied"), sem("v_first"), sem("v_rest_ready"), sem("v_second"), sem("v_ready"))
        p_high_ready, p_ready = sem("p_high_ready"), sem("p_ready")
        scores_ready, scores_copied, max_ready, exp_ready = sem("scores_ready"), sem("scores_copied"), sem("max_ready"), sem("exp_ready")
        top_ready, cut_ready = sem("top_ready"), [sem("cut0_ready"), sem("cut1_ready"), sem("cut2_ready")]
        sides_ready = [sem("sides0_ready"), sem("sides1_ready"), sem("sides2_ready")]
        cut_step, pick_step, found_ready, ok_step, ok_ready, ok_summed, ok_read = (
            sem("cut_step"), sem("pick_step"), sem("found_ready"), sem("ok_step"), sem("ok_ready"), sem("ok_summed"), sem("ok_read"))
        probs_ready, pt_ready, pt_copied, pv_done = sem("probs_ready"), sem("pt_ready"), sem("pt_copied"), sem("pv_done")
        cut_move_step = [sem("cut1_step"), sem("cut2_step")]
        inv_ready, o_ready, ot_ready, ot_copied = sem("inv_ready"), sem("o_ready"), sem("ot_ready"), sem("ot_copied")
        acc_ready, vare_ready, rstd_ready, norm_ready = sem("acc_ready"), sem("vare_ready"), sem("rstd_ready"), sem("norm_ready")
        nt_ready, nt_copied, moe_started = sem("nt_ready"), sem("nt_copied"), sem("moe_started")
        below_step, norm_step, route_step = sem("below_step"), sem("norm_step"), sem("route_step")
        logits_ready, centred, rexp_ready = sem("logits_ready"), sem("centred"), sem("rexp_ready")
        experts_loaded = [sem("even_expert_loaded"), sem("odd_expert_loaded")]
        gu_high_ready, gu_low_ready, row_high_ready, row_ready = (
            sem("gu_high_ready"), sem("gu_low_ready"), sem("row_high_ready"), sem("row_ready"))
        gu_ready, th_ready, hid_ready = sem("gu_ready"), sem("th_ready"), sem("hid_ready")
        act_ready, at_ready, at_copied, down_ready, moe_added = sem("act_ready"), sem("at_ready"), sem("at_copied"), sem("down_ready"), sem("moe_added")
        out_sent = sem("out_sent")
        block = ctx.enter_context(nc.Block())

        def stand_alone(eng, semaphore, value):
            value = eng.to_reg(value)
            eng.wait_ge(ident_set, 2)
            eng.wait_ge(semaphore, value)

        def self_attention(eng, b, period, finish=None):
            def run(first, last, r, j):
                period(first, last, (2 * b) * (PAIRS * TP) + r * (RING * GT), b * (PAIRS * TP) + r * (RING * GT),
                       b * (2 * PAIRS) + r * RING, (2 * b) * PAIRS + r * (RING // 2),
                       b * PAIRS + r * (RING // 2), r, j)
            for j in range(RING):
                run(True, False, 0, j)
                if finish and j < FINISH_STEPS:
                    finish(j)
            with eng.Fori(1, LOOPS - 1) as r:
                for j in range(RING):
                    run(False, False, r, j)
            for j in range(2 * RING):
                run(False, True, LOOPS - 1, j)

        FINISH_STEPS = 3

        def all_batches(eng, self_phase, cross_phase, finish):
            self_phase(0, None)
            with eng.Fori(1, B) as b:
                cross_phase(b - 1)
                self_phase(b, lambda j: finish(b - 1, j))
            cross_phase(B - 1)
            for j in range(FINISH_STEPS):
                finish(B - 1, j)

        def due(first, j, lag):
            return 0 <= j - lag < RING or (not first and j < lag)

        LAG_T, LAG_V = 2, 4

        def cross_attention(eng, b, slot):
            def run(first, last, r, t):
                slot(first, last, (2 * b + 1) * PAIRS + r * 2, b * (PAIRS * TP) + r * (2 * TP), r, t)
            for t in range(2 * TP):
                run(True, False, 0, t)
            with eng.Fori(1, LOOPS - 1) as r:
                for t in range(2 * TP):
                    run(False, False, r, t)
            for t in range(2 * TP + LAG_V + 2):
                run(False, True, LOOPS - 1, t)

        def live(first, t, lag):
            return 0 <= t - lag < 2 * TP or (not first and t < lag)

        def after_pair(first, t, slot):
            q = (t - slot) // TP - 1
            return q if (t - slot) % TP == 0 and (q >= 0 or not first) and -2 <= q < 2 and t >= slot else None

        @block.sync
        def _(sp):
            def load_inputs(b):
                sp.dma_start(x_T[:], xT[b].rearrange("c p t -> p c t")).then_inc(x_loaded, 16)
                sp.dma_start(ctx_T0[:], ctxT[b, 0:P, :]).then_inc(ctx_loaded, 16)
                sp.dma_start(ctx_T1[:], ctxT[b, P:CTX, :]).then_inc(ctx_loaded, 16)

            def load_rows(b):
                sp.dma_start(x1[:], x[b].rearrange("(n p) d -> p n d", p=P)).then_inc(res_loaded, 16)

            def load_pairs(w, g, r):
                for k in range(2):
                    sp.wait_ge(v_proj, g + k - 1)
                    sp.dma_start(w_pair[:, k], w[r * 2 + k]).then_inc(w_loaded[k], 16)

            def load_experts(ep):
                for k in range(2):
                    sp.dma_start(w_gu[:, k], w_gate_up[ep * 2 + k]).then_inc(experts_loaded[k], 16)
                    sp.dma_start(w_dn[:, k], w_down[ep * 2 + k]).then_inc(experts_loaded[k], 16)

            sp.dma_start(w_pair[:, 0], w_self[0]).then_inc(w_loaded[0], 16)
            load_inputs(0)
            sp.dma_start(w_pair[:, 1], w_self[1]).then_inc(w_loaded[1], 16)
            for dst, src in ((wo["self"], wo_self), (wo["cross"], wo_cross), (bo["self"], bo_self),
                             (bo["cross"], bo_cross), (gw, gate_wT)):
                sp.dma_start(dst[:], src).then_inc(const_loaded, 16)
            load_rows(0)
            with sp.Fori(1, PAIRS // 2) as r:
                load_pairs(w_self, r * 2, r)
            with sp.Fori(0, PAIRS // 2) as r:
                load_pairs(w_cross, r * 2 + PAIRS, r)
            with sp.Fori(1, B) as b:
                sp.wait_ge(v_proj, 2 * PAIRS * b)
                load_inputs(b)
                load_pairs(w_self, b * (2 * PAIRS), 0)
                sp.wait_ge(norm_ready, 2 * NT * b)
                load_rows(b)
                with sp.Fori(1, PAIRS // 2) as r:
                    load_pairs(w_self, b * (2 * PAIRS) + r * 2, r)
                with sp.Fori(0, PAIRS // 2) as r:
                    load_pairs(w_cross, b * (2 * PAIRS) + r * 2 + PAIRS, r)
            sp.wait_ge(norm_ready, (2 * B - 1) * NT)
            load_experts(0)
            with sp.Fori(1, E // 2) as ep:
                sp.wait_ge(down_ready, 2 * NU * ep)
                load_experts(ep)
            with sp.Fori(0, B) as b:
                sp.wait_ge(norm_ready, (2 * B + 1) * NT + b * NT)
                sp.dma_start(out[b].rearrange("(n p) d -> p n d", p=P), moe[:, bass.ds(b * NT, NT), :]).then_inc(out_sent, 16)
            sp.wait_ge(out_sent, 16 * B)

        @block.gpsimd
        def _(pool):
            nc.gpsimd.memset(ident[:], 0.0).then_inc(ident_set, 1)
            pool.wait_ge(ident_set, 1)
            nc.gpsimd.affine_select(out=ident[:], in_=ident[:], compare_op=ALU.not_equal, fill=1.0, base=0,
                                    pattern=[[-1, P]], channel_multiplier=1).then_inc(ident_set, 1)
            nc.gpsimd.memset(neg_half[:], -0.5).then_inc(consts_set, 1)
            nc.gpsimd.memset(ones_row[:], 1.0).then_inc(consts_set, 1)
            nc.gpsimd.memset(ones_col[:], 1.0).then_inc(consts_set, 1)
            nc.gpsimd.iota(places_i[:], [[0, GT], [1, WINDOW]], base=0, channel_multiplier=0).then_inc(consts_set, 1)
            pool.wait_ge(consts_set, 4)
            nc.gpsimd.tensor_copy(places[:], places_i[:]).then_inc(consts_set, 1)
            pool.wait_ge(consts_set, 5)

            TS, TT = nc.gpsimd.tensor_scalar, nc.gpsimd.tensor_tensor

            def move_cut(ns, gg, j, c):
                s_step = cut_move_step[c]
                stand_alone(pool, sides_ready[c], ns)
                TS(p_tmp[:, 2 * c + 2, :], sides[:, j, c, :], T - 2 * MOVES[c][1], -MOVES[c][0] / 2, ALU.add, ALU.mult).then_inc(s_step, 1)
                pool.wait_ge(s_step, 2 * gg - 1)
                TT(p_tmp[:, 2 * c + 3, :], p_tmp[:, 2 * c + 2, :], spread[:, j, :], ALU.mult).then_inc(s_step, 1)
                pool.wait_ge(s_step, 2 * gg)
                TT(neg_cut[:, j, c + 1, :], neg_cut[:, j, c, :], p_tmp[:, 2 * c + 3, :], ALU.add).then_inc(cut_ready[c + 1], 1)

            def split_probs(n, ns, i, fresh):
                stand_alone(pool, pt_copied, ns + 1)
                if not fresh:
                    stand_alone(pool, pv_done, n - 3)
                TS(p_high[:, i, :], p_T[:, i % 2, :], 1.0, 0.0, ALU.mult, ALU.add).then_inc(p_high_ready, 1)
                pool.wait_ge(p_high_ready, n + 1)
                TT(p_low[:, i, :], p_T[:, i % 2, :], p_high[:, i, :], ALU.subtract).then_inc(p_ready, 1)

            def value_part(q, k):
                return v_part[:, q, k].rearrange("p c d -> p (c d)")

            def first_value_part(g, gs, q):
                stand_alone(pool, v_copied, g + 1)
                TS(value_part(q, 0), v_sb[:], 1.0, 0.0, ALU.mult, ALU.add).then_inc(v_first, 1)
                pool.wait_ge(v_first, gs + 1)
                TT(v_rest[:], v_sb[:], value_part(q, 0), ALU.subtract).then_inc(v_rest_ready, 1)

            def last_value_parts(g, q):
                stand_alone(pool, v_rest_ready, g + 1)
                TS(value_part(q, 1), v_rest[:], 1.0, 0.0, ALU.mult, ALU.add).then_inc(v_second, 1)
                pool.wait_ge(v_second, g + 1)
                TT(value_part(q, 2), v_rest[:], value_part(q, 1), ALU.subtract).then_inc(v_ready, 1)

            def first_cut(ns, gg, j):
                stand_alone(pool, top_ready, ns)
                stand_alone(pool, scores_copied, ns)
                TS(neg_top[:, j, :], top8[:, j, :, 0], -1.0, None, ALU.mult).then_inc(cut_step, 1)
                TS(p_tmp[:, 0, :], s_sum[:, j, :], 1.0 / T, None, ALU.mult).then_inc(cut_step, 1)
                pool.wait_ge(cut_step, 4 * gg - 2)
                TT(spread[:, j, :], top8[:, j, :, 7], p_tmp[:, 0, :], ALU.subtract).then_inc(cut_step, 1)
                stand_alone(pool, cut_step, 4 * gg - 1)
                TS(p_tmp[:, 1, :], spread[:, j, :], -FIRST_CUT, None, ALU.mult).then_inc(cut_step, 1)
                pool.wait_ge(cut_step, 4 * gg)
                TT(neg_cut[:, j, 0, :], p_tmp[:, 1, :], p_tmp[:, 0, :], ALU.subtract).then_inc(cut_ready[0], 1)

            def judge(gg, j, fresh):
                stand_alone(pool, found_ready, gg)
                TS(p_tmp[:, 4, :], cut_sum[:, j, :], 2.0 / CUT, float(T), ALU.mult, ALU.add).then_inc(ok_step, 1)
                pool.wait_ge(ok_step, 3 * gg - 2)
                TT(p_tmp[:, 5, :], p_tmp[:, 4, :], sides[:, j, 2, :], ALU.add).then_inc(ok_step, 1)
                stand_alone(pool, ok_step, 3 * gg - 1)
                TS(p_tmp[:, 4, :], p_tmp[:, 5, :], 0.0, None, ALU.is_equal).then_inc(ok_step, 1)
                pool.wait_ge(ok_step, 3 * gg)
                if not fresh:
                    pool.wait_ge(ok_summed, gg - 1)
                TT(row_ok[:], p_tmp[:, 4, :], found[:, j, 0, :], ALU.mult).then_inc(ok_ready, 1)

            def period(first, last, nb, ns, gg, g, gs, r, j):
                new, cuts, low, old = (due(first, j, lag) for lag in range(4))

                def split(i):
                    split_probs(nb + (j - 3) * GT + i, ns + (j - 3) * GT + i, i, first and j == 3)

                if cuts:
                    move_cut(ns + j * GT, gg + j, (j - 1) % RING, 0)
                if old:
                    split(0)
                    split(1)
                if cuts:
                    move_cut(ns + j * GT, gg + j, (j - 1) % RING, 1)
                if old:
                    split(2)
                if low:
                    judge(gg + (j - 1), (j - 2) % RING, first and j == 2)
                if old:
                    split(3)
                if new:
                    first_cut(ns + (j + 1) * GT, gg + (j + 1), j)
                if new and j % 2 == 1:
                    first_value_part(g + j // 2, gs + j // 2, j // 2)
                    last_value_parts(g + j // 2, j // 2)

            def slot(first, last, g, nx, r, t):
                if t < 2 * TP and t % TP == 0:
                    last_value_parts(g + t // TP, t // TP)

            def rsqrt(n):
                pool.wait_ge(vare_ready, n + 1)
                nc.gpsimd.tensor_tensor(rstd[:], var_eps[:], neg_half[:, 0:NT], ALU.pow).then_inc(rstd_ready, 1)

            def self_phase(b, finish):
                self_attention(pool, b, period, finish)
                rsqrt(2 * b)

            def finish(b, j):
                if j == 1:
                    rsqrt(2 * b + 1)
                if j == 2:
                    pool.wait_ge(norm_ready, (2 * b + 2) * NT)
                    nc.gpsimd.tensor_copy(moe[:, bass.ds(b * NT, NT), :], x2_now).then_inc(moe_started, 1)

            all_batches(pool, self_phase, lambda b: cross_attention(pool, b, slot), finish)
            pool.wait_ge(vare_ready, 2 * B + 1)
            nc.gpsimd.tensor_tensor(last_rstd, last_var_eps, neg_half[:], ALU.pow).then_inc(rstd_ready, 1)

        @block.tensor
        def _(pe):
            def project_q(g, q):
                pe.wait_ge(w_loaded[q], 8 * (g - q) + 16)
                nc.tensor.matmul(proj[0][:], w_pair[:, q, 0, 0, :], x_T[:, 0, :], start=True, stop=False)
                nc.tensor.matmul(proj[0][:], w_pair[:, q, 0, 1, :], x_T[:, 1, :], start=False, stop=True).then_inc(q_proj, 1)

            def project_k(kind, q):
                in0, in1, w1 = ((x_T[:, 0, :], x_T[:, 1, :], w_pair[:, q, 1, 1, :]) if kind == "self" else
                                (ctx_T0[:], ctx_T1[:], w_pair[0:CTX1, q, 1, 1, :]))
                nc.tensor.matmul(proj[1][:], w_pair[:, q, 1, 0, :], in0, start=True, stop=False)
                nc.tensor.matmul(proj[1][:], w1, in1, start=False, stop=True).then_inc(k_proj, 1)

            def project_v(kind, q):
                w = w_pair[:, q]
                for c in range(NT):
                    tok = slice(c * P, (c + 1) * P)
                    if kind == "self":
                        in0, in1, w1 = x_T[:, 0, tok], x_T[:, 1, tok], w[:, 2, 1, :]
                    else:
                        in0, in1, w1 = ctx_T0[:, tok], ctx_T1[:, tok], w[0:CTX1, 2, 1, :]
                    nc.tensor.matmul(proj[0][:, tok], in0, w[:, 2, 0, :], start=True, stop=False)
                    last = nc.tensor.matmul(proj[0][:, tok], in1, w1, start=False, stop=True)
                last.then_inc(v_proj, 1)

            def scores(bank, q, h, i):
                rows, cols = slice(h * DH, (h + 1) * DH), slice(i * P, (i + 1) * P)
                nc.tensor.matmul(bank[:], q_low[rows, q, cols], k_high[rows, q, :], start=True, stop=False)
                nc.tensor.matmul(bank[:], q_high[rows, q, cols], k_low[rows, q, :], start=False, stop=False)
                nc.tensor.matmul(bank[:], q_high[rows, q, cols], k_high[rows, q, :], start=False, stop=True).then_inc(scores_ready, 1)

            def transpose_probs(bank, probs_tile):
                for c in range(NT):
                    last = nc.tensor.transpose(bank[:, c * P:(c + 1) * P], probs_tile[:, c * P:(c + 1) * P], ident[:])
                last.then_inc(pt_ready, 1)

            def weigh_values(bank, h, i, k, q):
                for c in range(NT):
                    at = slice(c * P, (c + 1) * P)
                    values = [v_part[:, q, m, c, h * DH:(h + 1) * DH] for m in range(3)]
                    for probs_part, value_part in ((p_low, 1), (p_low, 0), (p_high, 2), (p_high, 1), (p_high, 0)):
                        last = nc.tensor.matmul(bank[:, 2 * i + h, :], probs_part[:, k, at], values[value_part],
                                                start=(c == 0 and probs_part is p_low and value_part == 1),
                                                stop=(c == NT - 1 and probs_part is p_high and value_part == 0))
                last.then_inc(pv_done, 1)

            def turn_outputs():
                for c in range(NT):
                    last = nc.tensor.transpose(proj[1][:, c * P:(c + 1) * P], o_sb[:, 2 * c:2 * c + 2, :], ident[:])
                last.then_inc(ot_ready, 1)

            def project_out(kind, banks, copied, pairs, tiles=range(NT)):
                pe.wait_ge(const_loaded, 5 * 16)
                pe.wait_ge(ot_copied, copied)
                for i in tiles:
                    acc = banks[i // 2][:, (i % 2) * D:(i % 2 + 1) * D]
                    if pairs[0] == 0 and i % 2 == 0:
                        twice = bo[kind][:].rearrange("a (o d) -> a o d", o=1).to_broadcast([1, 2, D])
                        nc.tensor.matmul(banks[i // 2][:].rearrange("p (o d) -> p o d", o=2), ones_row[:], twice, start=True, stop=False)
                    for p in pairs:
                        last = nc.tensor.matmul(acc, o_T[:, p, i * P:(i + 1) * P], wo[kind][:, p, :],
                                                start=False, stop=(p == PAIRS - 1 and i % 2 == 1))
                if pairs[-1] == PAIRS - 1 and tiles[-1] == NT - 1:
                    last.then_inc(acc_ready, 1)

            def period(first, last, nb, ns, gg, g, gs, r, j):
                def tile(lag, i):
                    return (j - lag) * GT + i

                def scores_of(i):
                    if not (first and j == 0 and i < 2):
                        pe.wait_ge(scores_copied, ns + tile(0, i) - 1)
                    scores(sc[i % 2], j // 2, j % 2, i)

                def count_found():
                    pe.wait_ge(ok_ready, gg + (j - 2))
                    nc.tensor.matmul(ok_ps, ones_col[:], row_ok[:], start=True, stop=True).then_inc(ok_summed, 1)

                def turn(i):
                    pe.wait_ge(probs_ready, nb + tile(3, i) + 1)
                    if not (first and j == 3 and i < 2):
                        pe.wait_ge(pt_copied, ns + tile(3, i) - 1)
                    transpose_probs(pt[i % 2], p_sb[:, i, :])

                def weigh(lag, i):
                    pe.wait_ge(p_ready, nb + tile(lag, i) + 1)
                    weigh_values(o_ps, (j - lag) % 2, i, i, (j - lag) % RING // 2)

                new, old = due(first, j, 0), due(first, j, 3)
                if first and j == 0:
                    project_q(g, 0)
                    project_k("self", 0)
                if old and j % 2 == 0:
                    count_found()
                if new:
                    if j % 2 == 0:
                        pe.wait_ge(qk_ready, (g + j // 2) * 2 + 2)
                    scores_of(0)
                    scores_of(1)
                if old and j % 2 == 1:
                    count_found()
                if due(first, j, 4):
                    weigh(4, 2)
                    weigh(4, 3)
                if old:
                    turn(0)
                    turn(1)
                if j == RING:
                    pe.wait_ge(scores_copied, ns + RING * GT)
                    project_out("self", sc, g, range(PAIRS - 2), range(NT // 2))
                if j == RING + 1:
                    project_out("self", sc, g, range(PAIRS - 2), range(NT // 2, NT))
                if j == RING + 2:
                    project_out("self", sc, g + 1, (PAIRS - 2,))
                if new:
                    scores_of(2)
                    scores_of(3)
                    if j % 2 == 1:
                        project_v("self", j // 2)
                if old:
                    turn(2)
                    turn(3)
                ended = j % 2 == 1 and due(first, j - 1, 4)
                if ended:
                    pe.wait_ge(o_ready, g + (j - 3) // 2)
                    turn_outputs()
                if new and j % 2 == 1:
                    pe.wait_ge(v_copied, g + j // 2 + 1)
                    if not (last and j == RING - 1):
                        project_q(g + j // 2 + 1, (j // 2 + 1) % 2)
                        if ended:
                            pe.wait_ge(ot_copied, g + (j - 3) // 2)
                        project_k("self", (j // 2 + 1) % 2)
                if ended and not new:
                    pe.wait_ge(ot_copied, g + (j - 3) // 2)
                if old:
                    if j % 2 == 1:
                        pe.wait_ge(v_ready, g + (j - 3) // 2 + 1)
                        if ended:
                            pe.wait_ge(o_ready, g + (j - 3) // 2)
                    weigh(3, 0)
                    weigh(3, 1)

            def slot(first, last, g, nx, r, t):
                n = g * TP + t
                if first and t == 0:
                    project_q(g, 0)
                    project_k("cross", 0)
                if live(first, t, LAG_T):
                    pe.wait_ge(probs_ready, n - LAG_T + 1)
                    if not (first and t - LAG_T < 2):
                        pe.wait_ge(p_ready, n - LAG_T - 1)
                    transpose_probs(pt[t % 2], p_sb[:, (t - LAG_T) % 4, :])
                if t < 2 * TP:
                    if t % TP == 0:
                        pe.wait_ge(qk_ready, (g + t // TP) * 2 + 2)
                    if not (first and t < 2):
                        pe.wait_ge(probs_ready, n - 1)
                    scores(sc[t % 2], t // TP, t % TP // NT, t % NT)
                    if first and t == 0:
                        project_v("cross", 0)
                if live(first, t, LAG_V):
                    u = (t - LAG_V) % (2 * TP)
                    pe.wait_ge(p_ready, n - LAG_V + 1)
                    if u % TP == 0:
                        pe.wait_ge(v_ready, g + (t - LAG_V) // TP + 1)
                        if not first:
                            pe.wait_ge(o_ready, g + (t - LAG_V) // TP - 1)
                    weigh_values(outputs[u // TP], u % TP // NT, u % NT, u % 4, u // TP)
                if after_pair(first, t, LAG_V) is not None:
                    q = after_pair(first, t, LAG_V)
                    pe.wait_ge(o_ready, g + q + 1)
                    turn_outputs()
                if t < 2 * TP and not (last and t > TP):
                    if t % TP == TP - 4:
                        pe.wait_ge(v_rest_ready, g + t // TP + 1)
                        project_q(g + t // TP + 1, (t // TP + 1) % 2)
                    if t % TP == TP - 2:
                        if not (first and t < TP):
                            pe.wait_ge(ot_copied, g + t // TP)
                        project_k("cross", (t // TP + 1) % 2)
                    if t % TP == TP - 1:
                        pe.wait_ge(qk_ready, (g + t // TP + 1) * 2 + 1)
                        project_v("cross", (t // TP + 1) % 2)

            def turn_rows(phase, rows):
                pe.wait_ge(norm_ready, (phase + 1) * NT)
                for c in range(DC):
                    for i in range(NT):
                        last = nc.tensor.transpose(pt[c][:, i * P:(i + 1) * P], rows[:, i, c * P:(c + 1) * P], ident[:])
                last.then_inc(nt_ready, 1)

            pe.wait_ge(ident_set, 2)
            pe.wait_ge(consts_set, 5)
            def self_phase(b, finish):
                pe.wait_ge(x_loaded, 16 * b + 16)
                self_attention(pe, b, period, finish)
                project_out("self", sc, (2 * b + 1) * PAIRS, (PAIRS - 1,))
                turn_rows(2 * b, x1)

            def cross_phase(b):
                pe.wait_ge(ctx_loaded, 32 * b + 32)
                pe.wait_ge(nt_copied, (2 * b + 1) * DC)
                cross_attention(pe, b, slot)
                pe.wait_ge(ot_copied, (2 * b + 2) * PAIRS)

            def finish(b, j):
                if j == 0:
                    project_out("cross", pt, (2 * b + 2) * PAIRS, range(PAIRS), range(NT // 2))
                if j == 1:
                    project_out("cross", pt, (2 * b + 2) * PAIRS, range(PAIRS), range(NT // 2, NT))
                if j == 2:
                    turn_rows(2 * b + 1, x2_now)

            all_batches(pe, self_phase, cross_phase, finish)
            pe.wait_ge(nt_copied, 2 * B * DC)
            for i in range(NU):
                for c in range(DC):
                    last = nc.tensor.matmul(logits[:, i, :], x2_T[:, c, i, :], gw[:, c, :], start=(c == 0), stop=(c == DC - 1))
            last.then_inc(logits_ready, 1)

            gate_up, turned, down = sc, pt, proj
            with pe.Fori(0, E // 2) as ep:
                for j in range(2 * NU + 2):
                    n = ep * (2 * NU) + j
                    if j < 2 * NU:
                        k, i = j // NU, j % NU
                        if i == 0:
                            pe.wait_ge(gu_low_ready, (ep * 2 + k + 1) * DC)
                        pe.wait_ge(row_ready, n + 1)
                        if j >= 2:
                            pe.wait_ge(act_ready, n - 1)
                        for m, (rows, weights) in enumerate(((row_low, gu_high), (row_high, gu_low), (row_high, gu_high))):
                            for c in range(DC):
                                last = nc.tensor.matmul(gate_up[j % 2][:], rows[:, j % 2, c, :], weights[c][:, k, :],
                                                        start=(m == 0 and c == 0), stop=(m == 2 and c == DC - 1))
                        last.then_inc(gu_ready, 1)
                    if 0 <= j - 1 < 2 * NU:
                        pe.wait_ge(act_ready, n)
                        if j - 1 >= 2:
                            pe.wait_ge(at_copied, n - 2)
                        for c in range(FC):
                            last = nc.tensor.transpose(turned[(j - 1) % 2][:, c * P:(c + 1) * P],
                                                       act_sb[:, (j - 1) % 2, c * P:(c + 1) * P], ident[:])
                        last.then_inc(at_ready, 1)
                    if 0 <= j - 2 < 2 * NU:
                        k = (j - 2) // NU
                        pe.wait_ge(at_copied, n - 1)
                        if j - 2 >= 2:
                            pe.wait_ge(moe_added, n - 3)
                        if (j - 2) % NU == 0:
                            pe.wait_ge(experts_loaded[k], ep * 32 + 32)
                        for c in range(FC):
                            last = nc.tensor.matmul(down[j % 2][:, 0:D], act_T[:, j % 2, c * P:(c + 1) * P],
                                                    w_dn[:, k, c, :], start=(c == 0), stop=(c == FC - 1))
                        last.then_inc(down_ready, 1)

        @block.scalar
        def _(act):
            def copy_q(g, q, fresh):
                act.wait_ge(q_proj, g + 1)
                if not fresh:
                    act.wait_ge(scores_ready, (g - 1) * TP)
                nc.scalar.copy(q_high[:, q, :], proj[0][:]).then_inc(q_high_ready, 1)

            def copy_k(kind, g, q):
                act.wait_ge(k_proj, g + 1)
                nc.scalar.mul(k_high[:, q, :], proj[1][:], SCALE[kind]).then_inc(k_high_ready, 1)

            def copy_v(g, fresh):
                act.wait_ge(v_proj, g + 1)
                if not fresh:
                    act.wait_ge(v_rest_ready, g)
                nc.scalar.activation(v_sb[:], proj[0][:], ACT.Relu).then_inc(v_copied, 1)

            def copy_outputs(gn, p):
                act.wait_ge(ot_ready, gn)
                nc.scalar.mul(o_T[:, p, :], proj[1][:], 1.0 / P_SCALE).then_inc(ot_copied, 1)

            def period(first, last, nb, ns, gg, g, gs, r, j):
                def tile(lag, i):
                    return (j - lag) * GT + i

                def copy_scores(i):
                    act.wait_ge(scores_ready, nb + tile(0, i) + 1)
                    if not first:
                        act.wait_ge(probs_ready, nb + tile(4, i) + 1)
                    nc.scalar.activation(s_sb[:, j, i, :], sc[i % 2][:], ACT.Copy,
                                         accum_out=s_sum[:, j, i:i + 1]).then_inc(scores_copied, 1)

                def count(c, i):
                    jj = (j - 1) % RING
                    act.wait_ge(cut_ready[c], gg + j)
                    if c < 2:
                        ins = nc.scalar.activation(side_unused[:, i, :], s_sb[:, jj, i, :], ACT.Sign, bias=neg_cut[:, jj, c, i:i + 1],
                                                   scale=1.0, accum_out=sides[:, jj, c, i:i + 1])
                    else:
                        if not (first and j < 3):
                            act.wait_ge(below_step, 4 * (ns + tile(3, 0) + GT))
                        ins = nc.scalar.activation(side[:, jj % 2, i, :], s_sb[:, jj, i, :], ACT.Sign,
                                                   bias=neg_cut[:, jj, c, i:i + 1], scale=1.0, accum_out=sides[:, jj, c, i:i + 1])
                    ins.then_inc(sides_ready[c], 1)

                def exponential(i):
                    jj = (j - 3) % RING
                    if not (first and j == 3):
                        act.wait_ge(probs_ready, nb + tile(4, i) + 1)
                    nc.scalar.activation(e_sb[:, i, :], s_sb[:, jj, i, :], ACT.Exp, bias=neg_top[:, jj, i:i + 1],
                                         scale=1.0).then_inc(exp_ready, 1)

                def copy_turned(i):
                    act.wait_ge(pt_ready, nb + tile(3, i) + 1)
                    if not (first and j == 3 and i < 2):
                        act.wait_ge(p_ready, nb + tile(3, i) - 1)
                    nc.scalar.mul(p_T[:, i % 2, :], pt[i % 2][:], P_SCALE).then_inc(pt_copied, 1)

                new, cuts, old = due(first, j, 0), due(first, j, 1), due(first, j, 3)
                if first and j == 0:
                    copy_q(g, 0, True)
                    copy_k("self", g, 0)
                if old:
                    exponential(0)
                    exponential(1)
                if new:
                    copy_scores(0)
                    copy_scores(1)
                if old:
                    exponential(2)
                    exponential(3)
                if cuts:
                    for i in range(GT):
                        count(0, i)
                if new:
                    copy_scores(2)
                    copy_scores(3)
                if old:
                    copy_turned(0)
                    copy_turned(1)
                if new and j % 2 == 1:
                    copy_v(g + j // 2, first and j == 1)
                if cuts:
                    for i in range(GT):
                        count(1, i)
                if old:
                    copy_turned(2)
                    copy_turned(3)
                if j % 2 == 1 and due(first, j - 1, 4):
                    copy_outputs(g + (j - 3) // 2, r * 2 + (j - 5) // 2)
                following = new and j % 2 == 1 and not (last and j == RING - 1)
                if following:
                    copy_q(g + j // 2 + 1, (j // 2 + 1) % 2, first and j == 1)
                if cuts:
                    count(2, 0)
                    count(2, 1)
                if following:
                    copy_k("self", g + j // 2 + 1, (j // 2 + 1) % 2)
                if cuts:
                    count(2, 2)
                    count(2, 3)

            def slot(first, last, g, nx, r, t):
                n = g * TP + t
                if first and t == 0:
                    copy_q(g, 0, True)
                    copy_k("cross", g, 0)
                if live(first, t, LAG_T):
                    act.wait_ge(pt_ready, n - LAG_T + 1)
                    if not (first and t - LAG_T < 4):
                        act.wait_ge(pv_done, n - LAG_T - 3)
                    nc.scalar.mul(p_high[:, (t - LAG_T) % 4, :], pt[t % 2][:], P_SCALE).then_inc(p_high_ready, 1)
                if live(first, t, 1):
                    u = (t - 1) % (2 * TP)
                    act.wait_ge(max_ready, nx + t)
                    if not (first and t - 1 < 4):
                        act.wait_ge(pt_ready, n - 4)
                    if t % TP == 1 and not (first and t == 1):
                        act.wait_ge(inv_ready, g + t // TP)
                    at = 2 * (u % NT) + u % TP // NT
                    nc.scalar.activation(p_sb[:, u % 4, :], sc[u % 2][:], ACT.Exp,
                                         bias=neg_max[:, u % 4:u % 4 + 1], scale=1.0,
                                         accum_out=row_sum[:, at:at + 1]).then_inc(probs_ready, 1)
                if t < 2 * TP and t % TP == 0:
                    act.wait_ge(v_proj, g + t // TP + 1)
                    nc.scalar.copy(v_part[:, t // TP, 0].rearrange("p c d -> p (c d)"), proj[0][:]).then_inc(v_copied, 1)
                q = after_pair(first, t, LAG_V + 1)
                if q is not None:
                    copy_outputs(g + q + 1, r * 2 + q)
                if t < 2 * TP and not (last and t > TP):
                    if t % TP == TP - 3:
                        copy_q(g + t // TP + 1, (t // TP + 1) % 2, first and t < TP)
                    if t % TP == TP - 1:
                        copy_k("cross", g + t // TP + 1, (t // TP + 1) % 2)

            def self_phase(b, finish):
                self_attention(act, b, period, finish)
                act.wait_ge(nt_ready, 2 * b + 1)
                for c in range(DC):
                    nc.scalar.copy(x_T[:, c, :], pt[c][:]).then_inc(nt_copied, 1)

            def finish(b, j):
                if j == 2:
                    act.wait_ge(nt_ready, 2 * b + 2)
                    for c in range(DC):
                        nc.scalar.copy(x2_T[:, c, bass.ds(b * NT, NT), :].rearrange("p n t -> p (n t)"), pt[c][:]).then_inc(nt_copied, 1)
                    act.wait_ge(moe_started, b + 1)

            all_batches(act, self_phase, lambda b: cross_attention(act, b, slot), finish)
            act.wait_ge(centred, 1)
            nc.scalar.activation(probs[:], route[:], ACT.Exp).then_inc(rexp_ready, 1)

            def high_weights(ep, k):
                act.wait_ge(experts_loaded[k], ep * 32 + 32)
                for c in range(DC):
                    nc.scalar.copy(gu_high[c][:, k, :], w_gu[:, k, c, :]).then_inc(gu_high_ready, 1)

            def high_rows(j):
                nc.scalar.copy(row_high[:, j % 2], x2_T[:, :, j % NU, :]).then_inc(row_high_ready, 1)

            with act.Fori(0, E // 2) as ep:
                high_weights(ep, 0)
                high_rows(0)
                for j in range(2 * NU + 1):
                    n = ep * (2 * NU) + j
                    if j == SPLIT_AT:
                        high_weights(ep, 1)
                    if j < 2 * NU:
                        if j + 1 < 2 * NU:
                            if j >= 1:
                                act.wait_ge(gu_ready, n)
                            high_rows(j + 1)
                        act.wait_ge(gu_ready, n + 1)
                        if j >= 2:
                            act.wait_ge(hid_ready, n - 1)
                        nc.scalar.activation(th[:, j % 2, :], sc[j % 2][:, 0:F], ACT.Tanh, scale=0.5).then_inc(th_ready, 1)
                    if j >= 1:
                        act.wait_ge(at_ready, n)
                        if j - 1 >= 2:
                            act.wait_ge(down_ready, n - 2)
                        nc.scalar.copy(act_T[:, (j - 1) % 2, :], pt[(j - 1) % 2][:, 0:F]).then_inc(at_copied, 1)

        @block.vector
        def _(dve):
            def exact_search(jj, i):
                scores = s_sb[:, jj, i, :]
                for q in range(ROUNDS):
                    dve.drain()
                    nc.vector.max(best[:, q, :], scores)
                    dve.drain()
                    if q < ROUNDS - 1:
                        nc.vector.match_replace(exact[:, q % 2, :], best[:, q, :], scores, TAKEN)
                        scores = exact[:, q % 2, :]
                nc.vector.tensor_copy(found[:, jj, 1, i:i + 1], best[:, ROUNDS - 1, KTH:KTH + 1])
                dve.drain()

            def rest_of_q(g, q):
                dve.wait_ge(q_high_ready, g + 1)
                nc.vector.tensor_tensor(q_low[:, q, :], proj[0][:], q_high[:, q, :].bitcast(F32), ALU.subtract).then_inc(qk_ready, 1)

            def rest_of_k(kind, g, q):
                dve.wait_ge(k_high_ready, g + 1)
                nc.vector.scalar_tensor_tensor(out=k_low[:, q, :], in0=proj[1][:], scalar=SCALE[kind], in1=k_high[:, q, :].bitcast(F32),
                                               op0=ALU.mult, op1=ALU.subtract).then_inc(qk_ready, 1)

            def invert_sums(gn):
                dve.wait_ge(probs_ready, gn * TP)
                nc.vector.reciprocal(row_inv[:], row_sum[:]).then_inc(inv_ready, 1)

            def normalize(gn, bank):
                dve.wait_ge(pv_done, gn * TP)
                dve.wait_ge(inv_ready, gn)
                nc.vector.tensor_tensor(o_sb[:], bank[:], row_inv[:].rearrange("p (n o) -> p n o", o=1).to_broadcast([P, TP, DH]),
                                        ALU.mult).then_inc(o_ready, 1)

            def period(first, last, nb, ns, gg, g, gs, r, j):
                def tile(lag, i):
                    return (j - lag) * GT + i

                def top(i):
                    stand_alone(dve, scores_copied, ns + tile(0, i) + 1)
                    nc.vector.max(top8[:, j, i, :], s_sb[:, j, i, :]).then_inc(top_ready, 1)

                def next_below(i0):
                    jj = (j - 2) % RING
                    step = 4 * (ns + tile(2, i0))
                    for i in (i0, i0 + 1):
                        dve.wait_ge(sides_ready[2], ns + tile(2, i) + 1)
                        nc.vector.scalar_tensor_tensor(out=below[:, i % 2, :], in0=side[:, jj % 2, i, :], scalar=-CUT,
                                                       in1=s_sb[:, jj, i, :], op0=ALU.mult, op1=ALU.min,
                                                       accum_out=cut_sum[:, jj, i:i + 1]).then_inc(below_step, 1)
                    for i in (i0, i0 + 1):
                        stand_alone(dve, below_step, step + 1 + i % 2)
                        nc.vector.max(next16[:, i, 0:8], below[:, i % 2, :]).then_inc(below_step, 1)
                    for i in (i0, i0 + 1):
                        stand_alone(dve, below_step, step + 3 + i % 2)
                        nc.vector.match_replace(below2[:, i % 2, :], next16[:, i, 0:8], below[:, i % 2, :], TAKEN).then_inc(below_step, 1)
                    for i in (i0, i0 + 1):
                        stand_alone(dve, below_step, step + 5 + i % 2)
                        nc.vector.max(next16[:, i, 8:16], below2[:, i % 2, :]).then_inc(below_step, 1)

                def pick():
                    n, jj = gg + (j - 2), (j - 2) % RING
                    dve.wait_ge(below_step, 4 * (ns + tile(2, 0) + GT))
                    nc.vector.tensor_scalar(place[:], cut_sum[:, jj, :], 1.0 / CUT, float(K_TOP - 1), ALU.mult, ALU.add).then_inc(pick_step, 1)
                    dve.wait_ge(pick_step, 3 * n + 1)
                    nc.vector.tensor_tensor(picked[:, 0], places[:], place[:].rearrange("p (n o) -> p n o", o=1).to_broadcast([P, GT, WINDOW]),
                                            ALU.is_equal).then_inc(pick_step, 1)
                    dve.wait_ge(pick_step, 3 * n + 2)
                    nc.vector.tensor_tensor(picked[:, 1], picked[:, 0], next16[:], ALU.mult).then_inc(pick_step, 1)
                    dve.wait_ge(pick_step, 3 * n + 3)
                    nc.vector.tensor_reduce(found[:, jj], picked[:], AX.X, ALU.add).then_inc(found_ready, 1)

                def check():
                    n, jj = gg + (j - 3), (j - 3) % RING
                    dve.wait_ge(ok_summed, n + 1)
                    dve.wait_ge(found_ready, n + 1)
                    nc.vector.tensor_copy(rows_ok[0:1, 0:GT], ok_ps).then_inc(ok_read, 1)
                    nc.vector.tensor_reduce(rows_ok[0:1, GT:GT + 1], ok_ps, AX.X, ALU.min).then_inc(ok_read, 1)
                    stand_alone(dve, ok_read, 2 * n + 2)
                    least = dve.value_load(rows_ok[0:1, GT:GT + 1], min_val=0, max_val=P)
                    with dve.If(least < P):
                        for i in range(GT):
                            rows = dve.value_load(rows_ok[0:1, i:i + 1], min_val=0, max_val=P)
                            with dve.If(rows < P):
                                exact_search(jj, i)

                def mask(i):
                    jj = (j - 3) % RING
                    at = 2 * i + jj % 2
                    dve.wait_ge(exp_ready, ns + tile(3, i) + 1)
                    if not (first and j == 3):
                        dve.wait_ge(pt_ready, nb + tile(4, i) + 1)
                    nc.vector.scalar_tensor_tensor(out=p_sb[:, i, :], in0=s_sb[:, jj, i, :], scalar=found[:, jj, 1, i:i + 1],
                                                   in1=e_sb[:, i, :], op0=ALU.is_ge, op1=ALU.mult,
                                                   accum_out=row_sum[:, at:at + 1]).then_inc(probs_ready, 1)

                new, low, old = due(first, j, 0), due(first, j, 2), due(first, j, 3)
                ended = j % 2 == 1 and due(first, j - 1, 4)
                following = new and j % 2 == 1 and not (last and j == RING - 1)
                if first and j == 0:
                    rest_of_q(g, 0)
                    rest_of_k("self", g, 0)
                if ended:
                    invert_sums(g + (j - 3) // 2)
                if old:
                    check()
                    mask(0)
                    mask(1)
                if new:
                    top(0)
                    top(1)
                if low:
                    next_below(0)
                if ended:
                    normalize(g + (j - 3) // 2, o_ps)
                if old:
                    mask(2)
                    mask(3)
                if low:
                    next_below(2)
                    pick()
                if following:
                    rest_of_q(g + j // 2 + 1, (j // 2 + 1) % 2)
                if new:
                    top(2)
                    top(3)
                if following:
                    rest_of_k("self", g + j // 2 + 1, (j // 2 + 1) % 2)

            def slot(first, last, g, nx, r, t):
                n = g * TP + t
                if first and t == 0:
                    rest_of_q(g, 0)
                    rest_of_k("cross", g, 0)
                if t < 2 * TP:
                    dve.wait_ge(scores_ready, n + 1)
                    nc.vector.tensor_reduce(neg_max[:, t % 4:t % 4 + 1], sc[t % 2][:], AX.X, ALU.max, negate=True).then_inc(max_ready, 1)
                if live(first, t, LAG_T):
                    k = (t - LAG_T) % 4
                    dve.wait_ge(p_high_ready, n - LAG_T + 1)
                    nc.vector.scalar_tensor_tensor(out=p_low[:, k, :], in0=pt[t % 2][:], scalar=P_SCALE, in1=p_high[:, k, :],
                                                   op0=ALU.mult, op1=ALU.subtract).then_inc(p_ready, 1)
                if t < 2 * TP and t % TP == 0:
                    dve.wait_ge(v_copied, g + t // TP + 1)
                    if not (first and t == 0):
                        dve.wait_ge(v_ready, g + t // TP)
                    nc.vector.tensor_tensor(v_rest[:], proj[0][:], v_part[:, t // TP, 0].rearrange("p c d -> p (c d)"),
                                            ALU.subtract).then_inc(v_rest_ready, 1)
                q = after_pair(first, t, 0)
                if q is not None:
                    invert_sums(g + q + 1)
                q = after_pair(first, t, LAG_V - 1)
                if q is not None:
                    normalize(g + q + 1, outputs[q % 2])
                if t < 2 * TP and not (last and t > TP):
                    if t % TP == TP - 3:
                        rest_of_q(g + t // TP + 1, (t // TP + 1) % 2)
                    if t % TP == TP - 1:
                        rest_of_k("cross", g + t // TP + 1, (t // TP + 1) % 2)

            NSTEP = 2 + NT + NT

            def norm(m, add, dst):
                rows = add()
                dve.wait_ge(norm_step, m * NSTEP + 2)
                for i in range(NT):
                    nc.vector.bn_stats(stats[:, i, :], rows(i)).then_inc(norm_step, 1)
                for i in range(NT):
                    stand_alone(dve, norm_step, m * NSTEP + 2 + i + 1)
                    nc.vector.bn_aggr(mean_var[:, i, :], stats[:, i, :]).then_inc(norm_step, 1)
                dve.wait_ge(norm_step, m * NSTEP + NSTEP)
                nc.vector.tensor_scalar(var_eps[:], mean_var[:, :, 1], LN_EPS, None, ALU.add).then_inc(vare_ready, 1)
                dve.wait_ge(rstd_ready, m + 1)
                for i in range(NT):
                    nc.vector.tensor_scalar(dst(i), rows(i), mean_var[:, i, 0:1], rstd[:, i:i + 1],
                                            ALU.subtract, ALU.mult).then_inc(norm_ready, 1)

            def norm_attention(phase, banks, res, dst):
                def add():
                    dve.wait_ge(acc_ready, phase + 1)
                    for j in range(2):
                        nc.vector.tensor_tensor(y_sb[:, 2 * j:2 * j + 2, :].rearrange("p n d -> p (n d)"), banks[j][:],
                                                res[:, 2 * j:2 * j + 2, :].rearrange("p n d -> p (n d)"), ALU.add).then_inc(norm_step, 1)
                    return lambda i: y_sb[:, i, :]
                norm(phase, add, lambda i: dst[:, i, :])

            def self_phase(b, finish):
                self_attention(dve, b, period, finish)
                dve.wait_ge(res_loaded, 16 * b + 16)
                norm_attention(2 * b, sc, x1, x1)

            def finish(b, j):
                if j == 1:
                    norm_attention(2 * b + 1, pt, x1, x2_now)

            all_batches(dve, self_phase, lambda b: cross_attention(dve, b, slot), finish)

            steps = [0]

            def step(ins):
                ins.then_inc(route_step, 1)
                steps[0] += 1
                dve.wait_ge(route_step, steps[0])

            def wide(c):
                return c.rearrange("p (n o) -> p n o", o=1).to_broadcast([P, NU, E])

            dve.wait_ge(logits_ready, 1)
            step(nc.vector.tensor_reduce(col[:, 0, :], logits, AX.X, ALU.max))
            nc.vector.tensor_tensor(route[:], logits, wide(col[:, 0, :]), ALU.subtract).then_inc(centred, 1)
            dve.wait_ge(rexp_ready, 1)
            step(nc.vector.tensor_reduce(col[:, 1, :], probs[:], AX.X, ALU.add))
            step(nc.vector.reciprocal(col[:, 2, :], col[:, 1, :]))
            step(nc.vector.tensor_tensor(probs[:], probs[:], wide(col[:, 2, :]), ALU.mult))
            for i in range(NU):
                last = nc.vector.max(r_top[:, i, :], probs[:, i, :])
            step(last)
            second = r_top[:, :, TOP_EXPERTS - 1]
            step(nc.vector.tensor_copy(col[:, 3, :], second))
            step(nc.vector.tensor_tensor(above[:], probs[:], wide(col[:, 3, :]), ALU.is_gt))
            step(nc.vector.tensor_tensor(equal[:], probs[:], wide(col[:, 3, :]), ALU.is_equal))
            step(nc.vector.tensor_copy(rank[:, 0], equal[:]))
            shift, a = 1, 0
            while shift < E:
                step(nc.vector.tensor_copy(rank[:, (a + 1) % 3, :, 0:shift], rank[:, a, :, 0:shift]))
                step(nc.vector.tensor_tensor(rank[:, (a + 1) % 3, :, shift:E], rank[:, a, :, shift:E],
                                             rank[:, a, :, 0:E - shift], ALU.add))
                shift, a = 2 * shift, (a + 1) % 3
            step(nc.vector.tensor_reduce(col[:, 4, :], above[:], AX.X, ALU.add))
            step(nc.vector.tensor_scalar(col[:, 5, :], col[:, 4, :], -1.0, float(TOP_EXPERTS), ALU.mult, ALU.add))
            step(nc.vector.tensor_tensor(rank[:, a], rank[:, a], wide(col[:, 5, :]), ALU.is_le))
            step(nc.vector.tensor_tensor(equal[:], equal[:], rank[:, a], ALU.mult))
            step(nc.vector.tensor_tensor(above[:], above[:], equal[:], ALU.add))
            step(nc.vector.tensor_tensor(route[:], probs[:], above[:], ALU.mult))
            for again in range(2):
                step(nc.vector.tensor_reduce(col[:, 6, :], route[:], AX.X, ALU.add))
                step(nc.vector.tensor_scalar(col[:, 6, :], col[:, 6, :], ROUTE_EPS, None, ALU.add))
                step(nc.vector.reciprocal(col[:, 7, :], col[:, 6, :]))
                step(nc.vector.tensor_tensor(route[:], route[:], wide(col[:, 7, :]), ALU.mult))
            step(nc.vector.tensor_scalar(route[:], route[:], 0.5, None, ALU.mult))

            dve.wait_ge(moe_started, B)

            def low_weights(ep, k):
                for c in range(DC):
                    dve.wait_ge(gu_high_ready, (ep * 2 + k) * DC + c + 1)
                    nc.vector.tensor_tensor(gu_low[c][:, k, :], w_gu[:, k, c, :], gu_high[c][:, k, :].bitcast(F32),
                                            ALU.subtract).then_inc(gu_low_ready, 1)

            def low_rows(j, n):
                dve.wait_ge(row_high_ready, n + 1)
                nc.vector.tensor_tensor(row_low[:, j % 2], x2_T[:, :, j % NU, :], row_high[:, j % 2].bitcast(F32),
                                        ALU.subtract).then_inc(row_ready, 1)

            with dve.Fori(0, E // 2) as ep:
                low_weights(ep, 0)
                low_rows(0, ep * (2 * NU))
                for j in range(2 * NU + 2):
                    n = ep * (2 * NU) + j
                    if j == SPLIT_AT:
                        low_weights(ep, 1)
                    if j + 1 < 2 * NU:
                        low_rows(j + 1, n + 1)
                    if j < 2 * NU:
                        dve.wait_ge(th_ready, n + 1)
                        nc.vector.scalar_tensor_tensor(out=hid[:, j % 2, :], in0=th[:, j % 2, :], scalar=1.0,
                                                       in1=sc[j % 2][:, 0:F], op0=ALU.add, op1=ALU.mult).then_inc(hid_ready, 1)
                        dve.wait_ge(hid_ready, n + 1)
                        if j >= 2:
                            dve.wait_ge(at_ready, n - 1)
                        nc.vector.tensor_tensor(act_sb[:, j % 2, :], hid[:, j % 2, :], sc[j % 2][:, F:2 * F], ALU.mult).then_inc(act_ready, 1)
                    if j >= 2:
                        k, i = (j - 2) // NU, (j - 2) % NU
                        dve.wait_ge(down_ready, n - 1)
                        nc.vector.scalar_tensor_tensor(out=moe[:, i, :], in0=proj[j % 2][:, 0:D],
                                                       scalar=route[:, i, bass.ds(ep * 2 + k, 1)], in1=moe[:, i, :],
                                                       op0=ALU.mult, op1=ALU.add).then_inc(moe_added, 1)
            dve.wait_ge(moe_added, E * NU)
            done = 2 * B * NSTEP
            for i in range(NU):
                nc.vector.bn_stats(last_stats[:, i, :], moe[:, i, :]).then_inc(norm_step, 1)
            for i in range(NU):
                stand_alone(dve, norm_step, done + i + 1)
                nc.vector.bn_aggr(last_mean_var[:, i, :], last_stats[:, i, :]).then_inc(norm_step, 1)
            dve.wait_ge(norm_step, done + 2 * NU)
            nc.vector.tensor_scalar(last_var_eps, last_mean_var[:, :, 1], LN_EPS, None, ALU.add).then_inc(vare_ready, 1)
            dve.wait_ge(rstd_ready, 2 * B + 1)
            for i in range(NU):
                nc.vector.tensor_scalar(moe[:, i, :], moe[:, i, :], last_mean_var[:, i, 0:1], last_rstd[:, i:i + 1],
                                        ALU.subtract, ALU.mult).then_inc(norm_ready, 1)


def kernel(x, ctx_768, L0_attn_W_qkv, L0_attn_W_out, L0_attn_b_out, L0_xattn_w_q, L0_xattn_w_k, L0_xattn_w_v,
           L0_xattn_w_o, L0_xattn_b_o, L0_ffn_gate_w, L0_ffn_gate_up_proj, L0_ffn_down_proj):
    import numpy as np
    import concourse.bacc as bacc
    from concourse.bass_utils import run_bass_kernel_spmd

    x, ctx_768 = np.asarray(x), np.asarray(ctx_768)
    B, T, D = x.shape
    CTX = ctx_768.shape[2]
    INNER = L0_xattn_w_q.shape[1]
    PAIRS = INNER // P

    def pair_weights(q, k, v):
        w = np.zeros((PAIRS, P, 3, 2, P), np.float32)
        for n, m in enumerate((q, k, v)):
            for c in range(2):
                rows = np.asarray(m)[c * P:(c + 1) * P]
                w[:, :rows.shape[0], n, c, :] = rows.reshape(rows.shape[0], PAIRS, P).transpose(1, 0, 2)
        return w

    qkv = np.asarray(L0_attn_W_qkv).T
    arrays = {
        "xT": x.transpose(0, 2, 1).reshape(B, D // P, P, T),
        "x": x,
        "ctxT": ctx_768.transpose(0, 2, 1),
        "w_self": pair_weights(qkv[:, :INNER], qkv[:, INNER:2 * INNER], qkv[:, 2 * INNER:]),
        "wo_self": np.asarray(L0_attn_W_out).T.reshape(PAIRS, P, D).transpose(1, 0, 2),
        "bo_self": np.asarray(L0_attn_b_out).reshape(1, D),
        "w_cross": pair_weights(L0_xattn_w_q, L0_xattn_w_k, L0_xattn_w_v),
        "wo_cross": np.asarray(L0_xattn_w_o).reshape(PAIRS, P, D).transpose(1, 0, 2),
        "bo_cross": np.asarray(L0_xattn_b_o).reshape(1, D),
        "gate_wT": np.asarray(L0_ffn_gate_w).T.reshape(D // P, P, -1).transpose(1, 0, 2),
    }
    gu, dn = np.asarray(L0_ffn_gate_up_proj), np.asarray(L0_ffn_down_proj)
    arrays["w_gate_up"] = gu.reshape(gu.shape[0], D // P, P, -1).transpose(0, 2, 1, 3)
    arrays["w_down"] = dn.reshape(dn.shape[0], dn.shape[1] // P, P, D).transpose(0, 2, 1, 3)
    arrays = {n: np.ascontiguousarray(a) for n, a in arrays.items()}
    nc = bacc.Bacc("TRN2", target_bir_lowering=False, num_devices=1)
    args = [nc.dram_tensor(n, a.shape, mybir.dt.from_np(a.dtype), kind="ExternalInput").ap() for n, a in arrays.items()]
    args.append(nc.dram_tensor("out", x.shape, F32, kind="ExternalOutput").ap())
    decoder_kernel(nc, *args)
    r = run_bass_kernel_spmd(nc, [arrays], core_ids=[0])
    return r.results[0]["out"]
```
